# Optimizing a Trainium2 kernel written in Bass

```python
import numpy as np
import jax
import jax.numpy as jnp

def _softmax(x, axis=-1):
    return jax.nn.softmax(x, axis=axis)

def _gelu(x):
    return jax.nn.gelu(x, approximate=True)

def _silu(x):
    return jax.nn.silu(x)

def _sigmoid(x):
    return jax.nn.sigmoid(x)

def _layernorm(x, axis=-1, eps=1e-05):
    m = jnp.mean(x, axis=axis, keepdims=True)
    v = jnp.var(x, axis=axis, keepdims=True)
    return (x - m) / jnp.sqrt(v + eps)

def _scatter_add(tgt, idx, src, axis=0):
    return tgt.at[idx].add(src)

def _segment_sum(src, seg, n):
    return jax.ops.segment_sum(src, seg, n)
kernel_name = 'mk_decoder_postln_d1_seqx_r2_a24343'

def setup_inputs(seed: int=0):
    np.random.seed(seed)
    _w = jnp.asarray

    def _rec_inputs():
        import jax
        import jax.numpy as jnp
        _rk = jax.random.key(seed)
        x = -0.0002928 + 1 * jax.random.normal(jax.random.fold_in(_rk, 1), (8, 512, 512), jnp.float32)
        _lenS = 512 - jax.random.randint(jax.random.fold_in(_rk, 7), (8,), 0, max(1, 512 // 4) + 1, jnp.int32)
        _lenS2 = 77 - jax.random.randint(jax.random.fold_in(_rk, 8), (8,), 0, max(1, 77 // 4) + 1, jnp.int32)
        _ctx_1024P = jax.random.normal(jax.random.fold_in(_rk, 11), (8, 16, 512), jnp.float32)
        _ctx_1024c = jax.random.dirichlet(jax.random.fold_in(_rk, 511), 0.3 * jnp.ones((16,), jnp.float32), (8, 77))
        _ctx_1024t = jnp.einsum('bsk,bkd->bsd', _ctx_1024c, _ctx_1024P)
        _ctx_1024t = _ctx_1024t * jax.lax.rsqrt(jnp.mean(jnp.square(_ctx_1024t)) + 1e-12) * 0.953939
        ctx_1024 = -1.39393e-06 + 0.999914 * (_ctx_1024t + 0.3 * jax.random.normal(jax.random.fold_in(_rk, 611), (8, 77, 512), jnp.float32))
        _validS = jnp.arange(512)[None, :] < _lenS[:, None]
        _validS2 = jnp.arange(77)[None, :] < _lenS2[:, None]
        _causal = jnp.tril(jnp.ones((512, 512), dtype=bool))
        mask_SxS2_bk1 = jnp.broadcast_to(_validS2[0:1, :], (512, 77))
        mask_BxS2_bf0 = jnp.logical_not(jnp.ones((8, 77), dtype=bool))
        return (x, ctx_1024, mask_SxS2_bk1, mask_BxS2_bf0)
    x, ctx_1024, mask_SxS2_bk1, mask_BxS2_bf0 = _rec_inputs()

    def _L0_attn_setup():
        import jax, jax.numpy as jnp
        import numpy as np
        from math import ceil
        DIM = 512
        D_STATE = 16
        D_CONV = 4
        EXPAND = 2
        DI = DIM * EXPAND
        DT_RANK = ceil(DIM / 16)

        def _mamba(x, W_in, W_conv, b_conv, W_xproj, W_dt, b_dt, A_log, D, W_out):
            b, l, _ = x.shape
            silu = jax.nn.silu
            xr = x @ W_in.T
            xc, res = (xr[..., :DI], xr[..., DI:])
            u = jnp.transpose(xc, (0, 2, 1))
            u = jax.lax.conv_general_dilated(u, W_conv, window_strides=(1,), padding=[(D_CONV - 1, 0)], dimension_numbers=('NCH', 'OIH', 'NCH'), feature_group_count=DI)
            u = silu(u + b_conv[None, :, None])
            x_dbl = jnp.einsum('bdl,ed->ble', u, W_xproj)
            dt = x_dbl[..., :DT_RANK]
            B = x_dbl[..., DT_RANK:DT_RANK + D_STATE]
            C = x_dbl[..., DT_RANK + D_STATE:]
            delta = jax.nn.softplus(dt @ W_dt.T + b_dt)
            A = -jnp.exp(A_log)
            dA = jnp.exp(jnp.einsum('bld,dn->lbdn', delta, A))
            dBu = jnp.einsum('bld,bln,bdl->lbdn', delta, B, u)
            Cl = jnp.transpose(C, (1, 0, 2))

            def step(h, inp):
                dA_t, dBu_t, c_t = inp
                h = dA_t * h + dBu_t
                return (h, jnp.einsum('bdn,bn->bd', h, c_t))
            h0 = jnp.zeros((b, DI, D_STATE), u.dtype)
            _, ys = jax.lax.scan(step, h0, (dA, dBu, Cl))
            y = jnp.transpose(ys, (1, 2, 0)) + u * D[None, :, None]
            y = jnp.transpose(y, (0, 2, 1)) * silu(res)
            return y @ W_out.T
        key = jax.random.key(seed)
        ks = jax.random.split(key, 8)
        b, l = (2, 512)
        sc = lambda k, shp, s=0.02: jax.random.normal(k, shp, jnp.float32) * s
        x = jax.random.normal(ks[0], (b, l, DIM), jnp.float32)
        W_in = sc(ks[1], (2 * DI, DIM))
        W_conv = sc(ks[2], (DI, 1, D_CONV), 0.1)
        b_conv = jnp.zeros((DI,), jnp.float32)
        W_xproj = sc(ks[3], (DT_RANK + 2 * D_STATE, DI))
        W_dt = sc(ks[4], (DI, DT_RANK), 0.1)
        b_dt = jnp.zeros((DI,), jnp.float32)
        A_log = jnp.log(jnp.tile(jnp.arange(1, D_STATE + 1, dtype=jnp.float32)[None, :], (DI, 1)))
        D = jnp.ones((DI,), jnp.float32)
        W_out = sc(ks[5], (DIM, DI))
        return dict(x=x, W_in=W_in, W_conv=W_conv, b_conv=b_conv, W_xproj=W_xproj, W_dt=W_dt, b_dt=b_dt, A_log=A_log, D=D, W_out=W_out)
    _L0_attn_all = _L0_attn_setup()
    _L0_attn_in = {k: v for k, v in _L0_attn_all.items() if k in ('W_in', 'W_conv', 'b_conv', 'W_xproj', 'W_dt', 'b_dt', 'A_log', 'D', 'W_out')}
    del _L0_attn_all

    def _L0_xattn_setup():
        import jax, jax.numpy as jnp
        import numpy as np
        B, T, D, H = (2, 1024, 512, 16)
        DK = D // H
        SCALE = 1.0 / float(np.sqrt(DK))
        key0 = jax.random.key(seed)
        ks = jax.random.split(key0, 12)
        std = 0.02
        inp = {'query': jax.random.normal(ks[0], (B, T, D), jnp.float32), 'key': jax.random.normal(ks[1], (B, T, D), jnp.float32), 'value': jax.random.normal(ks[2], (B, T, D), jnp.float32), 'Wq': jax.random.normal(ks[3], (D, D), jnp.float32) * std, 'bq': jnp.zeros((D,), jnp.float32), 'Wk': jax.random.normal(ks[4], (D, D), jnp.float32) * std, 'bk': jnp.zeros((D,), jnp.float32), 'Wv': jax.random.normal(ks[5], (D, D), jnp.float32) * std, 'bv': jnp.zeros((D,), jnp.float32), 'Wo': jax.random.normal(ks[6], (D, D), jnp.float32) * std, 'bo': jnp.zeros((D,), jnp.float32), 'attn_mask': jnp.triu(jnp.ones((T, T), jnp.bool_), k=1), 'key_padding_mask': jnp.zeros((B, T), jnp.bool_)}
        return inp
    _L0_xattn_all = _L0_xattn_setup()
    _L0_xattn_in = {k: v for k, v in _L0_xattn_all.items() if k in ('Wq', 'bq', 'Wk', 'bk', 'Wv', 'bv', 'Wo', 'bo')}
    del _L0_xattn_all

    def _L0_ffn_setup():
        import jax, jax.numpy as jnp
        import numpy as np
        DIM = 512

        def _reference_tuple_inner(x, W_r, W_k, W_v, mu_r, mu_k):
            B, T, C = x.shape
            x_prev = jnp.concatenate([jnp.zeros((B, 1, C), x.dtype), x[:, :-1, :]], axis=1)
            xr = mu_r * x + (1.0 - mu_r) * x_prev
            xk = mu_k * x + (1.0 - mu_k) * x_prev
            r = jax.nn.sigmoid(jnp.einsum('btc,dc->btd', xr, W_r))
            k = jnp.einsum('btc,dc->btd', xk, W_k)
            k_act = jnp.square(jax.nn.relu(k))
            out = r * jnp.einsum('btc,dc->btd', k_act, W_v)
            new_state = x[:, -1, :]
            return (out, new_state)
        key = jax.random.key(seed)
        ks = jax.random.split(key, 6)
        B, T, C = (8, 1024, DIM)
        x = jax.random.normal(ks[0], (B, T, C), dtype=jnp.float32)
        s = 1.0 / np.sqrt(C)
        W_r = jax.random.uniform(ks[1], (C, C), jnp.float32, -s, s)
        W_k = jax.random.uniform(ks[2], (C, C), jnp.float32, -s, s)
        W_v = jax.random.uniform(ks[3], (C, C), jnp.float32, -s, s)
        mu_r = jax.random.uniform(ks[4], (C,), jnp.float32)
        mu_k = jax.random.uniform(ks[5], (C,), jnp.float32)
        return {'x': x, 'W_r': W_r, 'W_k': W_k, 'W_v': W_v, 'mu_r': mu_r, 'mu_k': mu_k}
    _L0_ffn_all = _L0_ffn_setup()
    _L0_ffn_in = {k: v for k, v in _L0_ffn_all.items() if k in ('W_r', 'W_k', 'W_v', 'mu_r', 'mu_k')}
    del _L0_ffn_all
    return {'x': x, 'ctx_1024': ctx_1024, 'mask_SxS2_bk1': mask_SxS2_bk1, 'mask_BxS2_bf0': mask_BxS2_bf0, 'L0_attn_W_in': _L0_attn_in['W_in'], 'L0_attn_W_conv': _L0_attn_in['W_conv'], 'L0_attn_b_conv': _L0_attn_in['b_conv'], 'L0_attn_W_xproj': _L0_attn_in['W_xproj'], 'L0_attn_W_dt': _L0_attn_in['W_dt'], 'L0_attn_b_dt': _L0_attn_in['b_dt'], 'L0_attn_A_log': _L0_attn_in['A_log'], 'L0_attn_D': _L0_attn_in['D'], 'L0_attn_W_out': _L0_attn_in['W_out'], 'L0_xattn_Wq': _L0_xattn_in['Wq'], 'L0_xattn_bq': _L0_xattn_in['bq'], 'L0_xattn_Wk': _L0_xattn_in['Wk'], 'L0_xattn_bk': _L0_xattn_in['bk'], 'L0_xattn_Wv': _L0_xattn_in['Wv'], 'L0_xattn_bv': _L0_xattn_in['bv'], 'L0_xattn_Wo': _L0_xattn_in['Wo'], 'L0_xattn_bo': _L0_xattn_in['bo'], 'L0_ffn_W_r': _L0_ffn_in['W_r'], 'L0_ffn_W_k': _L0_ffn_in['W_k'], 'L0_ffn_W_v': _L0_ffn_in['W_v'], 'L0_ffn_mu_r': _L0_ffn_in['mu_r'], 'L0_ffn_mu_k': _L0_ffn_in['mu_k']}

def reference(x, ctx_1024, mask_SxS2_bk1, mask_BxS2_bf0, L0_attn_W_in, L0_attn_W_conv, L0_attn_b_conv, L0_attn_W_xproj, L0_attn_W_dt, L0_attn_b_dt, L0_attn_A_log, L0_attn_D, L0_attn_W_out, L0_xattn_Wq, L0_xattn_bq, L0_xattn_Wk, L0_xattn_bk, L0_xattn_Wv, L0_xattn_bv, L0_xattn_Wo, L0_xattn_bo, L0_ffn_W_r, L0_ffn_W_k, L0_ffn_W_v, L0_ffn_mu_r, L0_ffn_mu_k):
    import jax
    import jax.numpy as jnp

    def _L0_attn_ref(x, W_in, W_conv, b_conv, W_xproj, W_dt, b_dt, A_log, D, W_out):
        import jax, jax.numpy as jnp
        import numpy as np
        from math import ceil
        DIM = 512
        D_STATE = 16
        D_CONV = 4
        EXPAND = 2
        DI = DIM * EXPAND
        DT_RANK = ceil(DIM / 16)

        def _mamba(x, W_in, W_conv, b_conv, W_xproj, W_dt, b_dt, A_log, D, W_out):
            b, l, _ = x.shape
            silu = jax.nn.silu
            xr = x @ W_in.T
            xc, res = (xr[..., :DI], xr[..., DI:])
            u = jnp.transpose(xc, (0, 2, 1))
            u = jax.lax.conv_general_dilated(u, W_conv, window_strides=(1,), padding=[(D_CONV - 1, 0)], dimension_numbers=('NCH', 'OIH', 'NCH'), feature_group_count=DI)
            u = silu(u + b_conv[None, :, None])
            x_dbl = jnp.einsum('bdl,ed->ble', u, W_xproj)
            dt = x_dbl[..., :DT_RANK]
            B = x_dbl[..., DT_RANK:DT_RANK + D_STATE]
            C = x_dbl[..., DT_RANK + D_STATE:]
            delta = jax.nn.softplus(dt @ W_dt.T + b_dt)
            A = -jnp.exp(A_log)
            dA = jnp.exp(jnp.einsum('bld,dn->lbdn', delta, A))
            dBu = jnp.einsum('bld,bln,bdl->lbdn', delta, B, u)
            Cl = jnp.transpose(C, (1, 0, 2))

            def step(h, inp):
                dA_t, dBu_t, c_t = inp
                h = dA_t * h + dBu_t
                return (h, jnp.einsum('bdn,bn->bd', h, c_t))
            h0 = jnp.zeros((b, DI, D_STATE), u.dtype)
            _, ys = jax.lax.scan(step, h0, (dA, dBu, Cl))
            y = jnp.transpose(ys, (1, 2, 0)) + u * D[None, :, None]
            y = jnp.transpose(y, (0, 2, 1)) * silu(res)
            return y @ W_out.T
        return _mamba(x, W_in, W_conv, b_conv, W_xproj, W_dt, b_dt, A_log, D, W_out)

    def _L0_xattn_ref(query, key, value, Wq, bq, Wk, bk, Wv, bv, Wo, bo, attn_mask, key_padding_mask):
        import jax, jax.numpy as jnp
        import numpy as np
        B, T, D, H = (2, 1024, 512, 16)
        DK = D // H
        SCALE = 1.0 / float(np.sqrt(DK))
        Bq, Tq, _ = query.shape
        Tk = key.shape[1]
        q = (query @ Wq.T + bq).reshape(Bq, Tq, H, DK)
        k = (key @ Wk.T + bk).reshape(Bq, Tk, H, DK)
        v = (value @ Wv.T + bv).reshape(Bq, Tk, H, DK)
        scores = jnp.einsum('bqhd,bkhd->bhqk', q, k) * jnp.float32(SCALE)
        neg_inf = jnp.float32(-jnp.inf)
        scores = jnp.where(attn_mask[None, None, :, :], neg_inf, scores)
        scores = jnp.where(key_padding_mask[:, None, None, :], neg_inf, scores)
        attn = jax.nn.softmax(scores, axis=-1)
        out = jnp.einsum('bhqk,bkhd->bqhd', attn, v).reshape(Bq, Tq, D)
        return out @ Wo.T + bo

    def _L0_ffn_ref(x, W_r, W_k, W_v, mu_r, mu_k):
        import jax, jax.numpy as jnp
        import numpy as np
        DIM = 512

        def _reference_tuple_inner(x, W_r, W_k, W_v, mu_r, mu_k):
            B, T, C = x.shape
            x_prev = jnp.concatenate([jnp.zeros((B, 1, C), x.dtype), x[:, :-1, :]], axis=1)
            xr = mu_r * x + (1.0 - mu_r) * x_prev
            xk = mu_k * x + (1.0 - mu_k) * x_prev
            r = jax.nn.sigmoid(jnp.einsum('btc,dc->btd', xr, W_r))
            k = jnp.einsum('btc,dc->btd', xk, W_k)
            k_act = jnp.square(jax.nn.relu(k))
            out = r * jnp.einsum('btc,dc->btd', k_act, W_v)
            new_state = x[:, -1, :]
            return (out, new_state)
        return _reference_tuple_inner(x, W_r, W_k, W_v, mu_r, mu_k)[0]
    x = _layernorm(x + _L0_attn_ref(x, L0_attn_W_in, L0_attn_W_conv, L0_attn_b_conv, L0_attn_W_xproj, L0_attn_W_dt, L0_attn_b_dt, L0_attn_A_log, L0_attn_D, L0_attn_W_out), axis=-1)
    x = _layernorm(x + _L0_xattn_ref(x, ctx_1024, ctx_1024, L0_xattn_Wq, L0_xattn_bq, L0_xattn_Wk, L0_xattn_bk, L0_xattn_Wv, L0_xattn_bv, L0_xattn_Wo, L0_xattn_bo, mask_SxS2_bk1, mask_BxS2_bf0), axis=-1)
    x = _layernorm(x + _L0_ffn_ref(x, L0_ffn_W_r, L0_ffn_W_k, L0_ffn_W_v, L0_ffn_mu_r, L0_ffn_mu_k), axis=-1)
    return x

_drawn_inputs = setup_inputs


def setup_inputs(seed=0):
    import zlib

    import numpy as np

    out = dict(_drawn_inputs(seed))
    spreads = {'L0_attn_b_conv': (0.0, 0.79),
     'L0_attn_b_dt': (0.0, 0.8),
     'L0_attn_D': (1.0, 0.6),
     'L0_xattn_bq': (0.0, 0.8),
     'L0_xattn_bk': (0.0, 0.8),
     'L0_xattn_bv': (0.0, 0.1),
     'L0_xattn_bo': (0.0, 0.1)}
    factors = {'L0_attn_W_in': 4.575,
     'L0_attn_W_conv': 6.17,
     'L0_attn_W_xproj': 8.0,
     'L0_attn_W_dt': 8.0,
     'L0_attn_A_log': 8.0,
     'L0_attn_W_out': 4.136,
     'L0_xattn_Wq': 4.059,
     'L0_xattn_Wk': 4.036,
     'L0_ffn_W_r': 3.121,
     'L0_ffn_mu_r': 6.542}
    for name, (base, spread) in spreads.items():
        noise = np.random.default_rng([zlib.crc32(name.encode()), seed]).standard_normal(out[name].shape)
        drawn = base * np.exp(spread * noise) if base else spread * noise
        out[name] = jnp.asarray(drawn.astype(out[name].dtype))
    for name, factor in factors.items():
        out[name] = (out[name] * factor).astype(out[name].dtype)
    return out
```

```python
import concourse.bass as bass
from concourse import mybir
from contextlib import ExitStack

FP32 = mybir.dt.float32
U8 = mybir.dt.uint8
ALU = mybir.AluOpType
ACT = mybir.ActivationFunctionType
AX = mybir.AxisListType

P = 128
EPS = 1e-5


def mamba_pass(nc, x, x_t, c_dram, w_in, w_conv, b_conv, w_x, w_dt, a_log, d_skip, w_out, ident_d, x1):
    NB, T, DM = x.shape
    DI = w_in.shape[2] // 2
    NS = a_log.shape[2]
    KT = DM // P
    ND = DI // P
    TT = T // P
    TAPS = w_conv.shape[2]
    DTR = 32
    B0, C0 = DTR + 1, DTR + 1 + NS
    NU = NS // 2
    NP = NU // 2
    LEAD = 2
    LN_SLACK = 3e-10

    ctx = ExitStack()
    with ctx:
        def sb(name, shape, dt=FP32):
            return ctx.enter_context(nc.sbuf_tensor("mamba_" + name, shape, dt))

        def sem(name):
            return ctx.enter_context(nc.semaphore(name))

        win = sb("win", [P, KT, 2 * DI])
        wout = sb("wout", [P, ND, DM])
        wx = sb("wx", [P, ND, P])
        wdt = sb("wdt", [P, DI])
        wcv = sb("wcv", [P, ND, TAPS])
        bcv = sb("bcv", [P, ND])
        a_neg = sb("a_neg", [P, ND, NS])
        dsk = sb("dsk", [P, ND])
        ident = sb("ident", [P, P])
        eps = sb("eps", [P, 1])
        tick = sb("tick", [P, 1])
        u = sb("u", [P, ND, T])
        gate = sb("gate", [P, ND, T])
        diag_b = sb("diag_b", [P, TT, NS, P])
        c_row = sb("c_row", [P, NS, T])
        xdbl = sb("xdbl", [P, T])
        b_col = sb("b_col", [P, TT, NS])
        wdt_s = [sb(f"wdt_s{i}", [P, P]) for i in range(2)]
        sp_e = sb("sp_e", [P, T])
        sp_l = sb("sp_l", [P, T])
        sp_s = sb("sp_s", [P, T])
        delta = [sb(f"delta{i}", [P, T]) for i in range(2)]
        v = sb("v", [P, T])
        v_t = [sb(f"v_t{i}", [P, T]) for i in range(2)]
        ring = sb("ring", [P, NU, 2, T])
        xt = ring[:, 4:6].rearrange("p a b t -> p (a b) t")
        zero2 = sb("zero2", [P, 2, 1])
        st6 = sb("st6", [P, TT, 6])
        mv = sb("mv", [P, TT, 2])
        rstd = sb("rstd", [P, TT])

        ps = ctx.enter_context(nc.psum_tensor("ps", [P, 8, T], FP32))
        BT_BANK, DT_BANK = 6, 7

        w_loaded = sem("w_loaded")
        a_exp = sem("a_exp")
        consts = sem("consts")
        xt_loaded = sem("xt_loaded")
        u_proj = sem("u_proj")
        tap_last = sem("tap_last")
        taps = sem("taps")
        u_ready = sem("u_ready")
        x_proj = sem("x_proj")
        xdbl_ready = sem("xdbl_ready")
        bt_proj = sem("bt_proj")
        bcol_ready = sem("bcol_ready")
        diag_dve = sem("diag_dve")
        diag_pool = sem("diag_pool")
        c_stored = sem("c_stored")
        c_loaded = sem("c_loaded")
        r_proj = sem("r_proj")
        r_taken = sem("r_taken")
        wdt_ready = sem("wdt_ready")
        dt_proj = sem("dt_proj")
        sp = sem("sp")
        sq = sem("sq")
        delta_ready = sem("delta_ready")
        v_ready = sem("v_ready")
        vt_proj = sem("vt_proj")
        vt_ready = sem("vt_ready")
        da_ready = sem("da_ready")
        dbu_ready = sem("dbu_ready")
        scanned = sem("scanned")
        c_pool = sem("c_pool")
        c_dve = sem("c_dve")
        paired = sem("paired")
        folded = sem("folded")
        summed = sem("summed")
        y_taken = sem("y_taken")
        yg_ready = sem("yg_ready")
        x_loaded = sem("x_loaded")
        o_proj = sem("o_proj")
        z_done = sem("z_done")
        stats = sem("stats")
        rstd_ln = sem("rstd_ln")
        rstd_ready = sem("rstd_ready")
        normed = sem("normed")
        stored = sem("stored")

        N_W = 9
        block = ctx.enter_context(nc.Block())

        @block.sync
        def _(sp_eng):
            for dst, src in ((ident, ident_d), (wcv, w_conv), (bcv, b_conv), (win, w_in), (a_neg, a_log),
                             (dsk, d_skip), (wx, w_x), (wdt, w_dt), (wout, w_out)):
                sp_eng.dma_start(dst[:], src).then_inc(w_loaded, 16)
            sp_eng.dma_start(xt, x_t[0]).then_inc(xt_loaded, 16)

            def row(b, last=False):
                sp_eng.wait_ge(xdbl_ready, b + 1)
                sp_eng.dma_start(c_dram, xdbl[C0:C0 + NS, :]).then_inc(c_stored, 16)
                sp_eng.wait_ge(c_stored, b * 16 + 16)
                sp_eng.dma_start(c_row[:], c_dram.unsqueeze(0).broadcast_to([P, NS, T])).then_inc(c_loaded, 16)
                sp_eng.wait_ge(summed, b * (ND * NP) + ND * NP + NP)
                if not last:
                    sp_eng.dma_start(xt, x_t[b + 1]).then_inc(xt_loaded, 16)
                for tb in range(TT):
                    sp_eng.dma_start(ring[:, tb, 0, :], x[b, tb * P:(tb + 1) * P, :]).then_inc(x_loaded, 16)
                for tb in range(TT):
                    sp_eng.wait_ge(normed, b * TT + tb + 1)
                    sp_eng.dma_start(x1[b, tb * P:(tb + 1) * P, :], ring[:, tb, 0, :]).then_inc(stored, 16)

            sp_eng.nop().then_inc(stored, 16)
            with sp_eng.Fori(0, NB - 1) as b:
                row(b)
            row(NB - 1, last=True)
            sp_eng.wait_ge(stored, NB * TT * 16 + 16)

        @block.tensor
        def _(pe):
            pe.wait_ge(w_loaded, 16 * N_W)

            def dt_product(b, d, par):
                pe.wait_ge(wdt_ready, b * ND + d + 1)
                nc.tensor.matmul(ps[:, DT_BANK, :], wdt_s[par][:], xdbl[:], start=True,
                                 stop=True).then_inc(dt_proj, 1)

            def v_transposes(b, d):
                pe.wait_ge(v_ready, b * ND + d + 1)
                for tb in range(TT):
                    m = nc.tensor.transpose(ps[:, BT_BANK, tb * P:(tb + 1) * P], v[:, tb * P:(tb + 1) * P],
                                            ident[:])
                m.then_inc(vt_proj, 1)

            def b_products(b, d, par, k):
                s = k % 2
                if k == 0:
                    pe.wait_ge(vt_ready, b * ND + d + 1)
                pe.wait_ge(scanned, b * (ND * NU) + d * NU + k + 1)
                for tb in range(TT):
                    for i in range(2):
                        m = nc.tensor.matmul(ps[:, 2 * s + i, tb * P:(tb + 1) * P],
                                             v_t[par][:, tb * P:(tb + 1) * P], diag_b[:, tb, 2 * k + i, :],
                                             start=True, stop=True)
                m.then_inc(dbu_ready, 1)

            def state_sum(b, d, par, p):
                if p == 0:
                    pe.wait_ge(y_taken, b * ND + d + 1)
                pe.wait_ge(folded, b * (ND * NP) + d * NP + p + 1)
                nc.tensor.matmul(ps[:, 4 + par, :], ident[:], ring[:, 2 * p, 0, :], start=(p == 0),
                                 stop=(p == NP - 1)).then_inc(summed, 1)

            def step(b, d, par, p, nxt=True, more=True):
                if p + LEAD < NP:
                    b_products(b, d, par, 2 * (p + LEAD))
                    b_products(b, d, par, 2 * (p + LEAD) + 1)
                elif nxt:
                    b_products(b, d + 1, 1 - par, 2 * (p + LEAD - NP))
                    b_products(b, d + 1, 1 - par, 2 * (p + LEAD - NP) + 1)
                if p == 1 and nxt:
                    v_transposes(b, d + 1)
                state_sum(b, d, par, p)
                if p == 1 and more:
                    dt_product(b, d + 2, par)

            def channel_block(b, d, par, nxt=True, more=True):
                for p in range(1, NP):
                    step(b, d, par, p, nxt, more)
                if nxt:
                    step(b, d + 1, 1 - par, 0)

            nc.tensor.nop().then_inc(summed, NP)
            with pe.Fori(0, NB) as b:
                pe.wait_ge(xt_loaded, b * 16 + 16)
                for j in range(ND):
                    if j >= 4:
                        pe.wait_ge(taps, b * (ND * (TAPS - 1)) + (j - 3) * (TAPS - 1))
                    for kt in range(KT):
                        m = nc.tensor.matmul(ps[:, j % 4, :], win[:, kt, j * P:(j + 1) * P], xt[:, kt, :],
                                             start=(kt == 0), stop=(kt == KT - 1))
                    m.then_inc(u_proj, 1)
                for j in range(ND):
                    pe.wait_ge(u_ready, b * ND + j + 1)
                    m = nc.tensor.matmul(ps[:, BT_BANK, :], wx[:, j, :], u[:, j, :], start=(j == 0),
                                         stop=(j == ND - 1))
                m.then_inc(x_proj, 1)
                pe.wait_ge(xdbl_ready, b + 1)
                for tb in range(TT):
                    m = nc.tensor.matmul(ps[:, BT_BANK, tb * P:tb * P + NS], xdbl[:, tb * P:(tb + 1) * P],
                                         ident[:, B0:B0 + NS], start=True, stop=True)
                m.then_inc(bt_proj, 1)
                dt_product(b, 0, 0)
                for j in range(ND):
                    if j >= 4:
                        pe.wait_ge(r_taken, b * ND + j - 3)
                    for kt in range(KT):
                        m = nc.tensor.matmul(ps[:, j % 4, :], win[:, kt, DI + j * P:DI + (j + 1) * P],
                                             xt[:, kt, :], start=(kt == 0), stop=(kt == KT - 1))
                    m.then_inc(r_proj, 1)
                    if j == 3:
                        pe.wait_ge(bcol_ready, b + 1)
                        v_transposes(b, 0)
                        dt_product(b, 1, 1)
                pe.wait_ge(r_taken, b * ND + ND)
                pe.wait_ge(diag_dve, b * 2 + 2)
                pe.wait_ge(diag_pool, b * 2 + 2)
                for k in range(2 * LEAD):
                    b_products(b, 0, 0, k)
                step(b, 0, 0, 0)
                with pe.Fori(0, ND // 2 - 1) as j:
                    for par in range(2):
                        channel_block(b, j * 2 + par, par)
                channel_block(b, ND - 2, 0, more=False)
                channel_block(b, ND - 1, 1, nxt=False, more=False)
                pe.wait_ge(yg_ready, b * ND + ND)
                for tb in range(TT):
                    if tb >= 2:
                        pe.wait_ge(z_done, b * TT + tb - 1)
                    for d in range(ND):
                        m = nc.tensor.matmul(ps[:, 6 + tb % 2, :], gate[:, d, tb * P:(tb + 1) * P], wout[:, d, :],
                                             start=(d == 0), stop=(d == ND - 1))
                    m.then_inc(o_proj, 1)

        @block.scalar
        def _(act):
            act.wait_ge(w_loaded, 16 * N_W)
            nc.scalar.activation(a_neg[:], a_neg[:], ACT.Exp).then_inc(a_exp, 1)
            act.wait_ge(consts, 3)

            def softplus(b, d):
                act.wait_ge(dt_proj, b * ND + d + 1)
                if not (isinstance(d, int) and d == 0):
                    act.wait_ge(delta_ready, b * ND + d)
                nc.scalar.activation(sp_e[:], ps[:, DT_BANK, :], ACT.Abs).then_inc(sp, 1)
                act.wait_ge(sp, b * (4 * ND) + d * 4 + 1)
                nc.scalar.activation(sp_e[:], sp_e[:], ACT.Exp, scale=-1.0).then_inc(sp, 1)
                act.wait_ge(sp, b * (4 * ND) + d * 4 + 2)
                nc.scalar.activation(sp_l[:], sp_e[:], ACT.Ln, bias=1.0).then_inc(sp, 1)
                nc.scalar.activation(sp_s[:], sp_e[:], ACT.Square, scale=0.5 ** 0.5).then_inc(sp, 1)

            def take_vt(b, d, par):
                act.wait_ge(vt_proj, b * ND + d + 1)
                nc.scalar.copy(v_t[par][:], ps[:, BT_BANK, :]).then_inc(vt_ready, 1)

            def decay(b, d, par, k):
                if k == 0:
                    act.wait_ge(delta_ready, b * ND + d + 1)
                if k % 2 == 0:
                    act.wait_ge(summed, b * (ND * NP) + d * NP + k // 2 + 1)
                nc.scalar.copy(ring[:, k, :, 0:1], zero2[:])
                for i in range(2):
                    a = nc.scalar.activation(ring[:, k, i, 1:], delta[par][:, 1:], ACT.Exp,
                                             scale=a_neg[:, d, 2 * k + i:2 * k + i + 1])
                a.then_inc(da_ready, 1)

            def step(b, d, par, p, nxt=True, more=True):
                if p == 2 and more:
                    softplus(b, d + 2)
                if p + LEAD < NP:
                    decay(b, d, par, 2 * (p + LEAD))
                    decay(b, d, par, 2 * (p + LEAD) + 1)
                elif nxt:
                    decay(b, d + 1, 1 - par, 2 * (p + LEAD - NP))
                    decay(b, d + 1, 1 - par, 2 * (p + LEAD - NP) + 1)
                if p == 1 and nxt:
                    take_vt(b, d + 1, 1 - par)

            def channel_block(b, d, par, nxt=True, more=True):
                for p in range(1, NP):
                    step(b, d, par, p, nxt, more)
                if nxt:
                    step(b, d + 1, 1 - par, 0)

            with act.Fori(0, NB) as b:
                def silu_u(j):
                    act.wait_ge(taps, b * (ND * (TAPS - 1)) + (j + 1) * (TAPS - 1))
                    nc.scalar.activation(u[:, j, :], u[:, j, :], ACT.Silu).then_inc(u_ready, 1)

                for j in range(ND):
                    act.wait_ge(u_proj, b * ND + j + 1)
                    nc.scalar.activation(u[:, j, :], ps[:, j % 4, :], ACT.Identity, bias=bcv[:, j:j + 1],
                                         scale=wcv[:, j, TAPS - 1:TAPS]).then_inc(tap_last, 1)
                    if j >= 1:
                        silu_u(j - 1)
                silu_u(ND - 1)
                act.wait_ge(x_proj, b + 1)
                nc.scalar.activation(xdbl[:], ps[:, BT_BANK, :], ACT.Identity,
                                     bias=ident[:, DTR:DTR + 1]).then_inc(xdbl_ready, 1)
                softplus(b, 0)
                for j in range(ND):
                    act.wait_ge(r_proj, b * ND + j + 1)
                    nc.scalar.activation(gate[:, j, :], ps[:, j % 4, :], ACT.Silu).then_inc(r_taken, 1)
                take_vt(b, 0, 0)
                softplus(b, 1)
                act.wait_ge(stored, b * (16 * TT) + 16)
                for k in range(2 * LEAD):
                    decay(b, 0, 0, k)
                step(b, 0, 0, 0)
                with act.Fori(0, ND // 2 - 1) as j:
                    for par in range(2):
                        channel_block(b, j * 2 + par, par)
                channel_block(b, ND - 2, 0, more=False)
                channel_block(b, ND - 1, 1, nxt=False, more=False)
                act.wait_ge(stats, b * (2 * TT) + 2 * TT)
                nc.scalar.activation(rstd[:], mv[:, :, 1], ACT.Ln, bias=eps[:]).then_inc(rstd_ln, 1)
                act.wait_ge(rstd_ln, b + 1)
                nc.scalar.activation(rstd[:], rstd[:], ACT.Exp, scale=-0.5).then_inc(rstd_ready, 1)

        @block.vector
        def _(dve):
            dve.wait_ge(a_exp, 1)
            nc.vector.tensor_scalar(a_neg[:], a_neg[:], -1.0, None, ALU.mult).then_inc(consts, 1)
            nc.vector.memset(eps[:], EPS).then_inc(consts, 1)
            nc.vector.memset(zero2[:], 0.0).then_inc(consts, 1)
            dve.wait_ge(consts, 3)
            nc.vector.nop().then_inc(scanned, 2)
            nc.vector.nop().then_inc(y_taken, 2)

            def scan(b, d, par, k):
                dve.wait_ge(dbu_ready, b * (ND * NU) + d * NU + k + 1)
                dve.wait_ge(da_ready, b * (ND * NU) + d * NU + k + 1)
                s = k % 2
                slot = ring[:, k].rearrange("p a t -> p (a t)")
                nc.vector.tensor_tensor_scan(slot, slot, ps[:, 2 * s:2 * s + 2, :].rearrange("p a t -> p (a t)"),
                                             0.0, ALU.mult, ALU.add).then_inc(scanned, 1)

            def times_c(b, d, p):
                k = 2 * p + 1
                if p == 0 and isinstance(d, int) and d == 0:
                    dve.wait_ge(c_loaded, b * 16 + 16)
                dve.wait_ge(scanned, b * (ND * NU) + d * NU + k + 3)
                nc.vector.tensor_tensor(ring[:, k], ring[:, k], c_row[:, 2 * k:2 * k + 2, :],
                                        ALU.mult).then_inc(c_dve, 1)

            def fold(b, d, p):
                dve.wait_ge(paired, b * (ND * NP) + d * NP + p + 1)
                nc.vector.tensor_tensor(ring[:, 2 * p, 0, :], ring[:, 2 * p, 0, :], ring[:, 2 * p, 1, :],
                                        ALU.add).then_inc(folded, 1)

            def softplus(b, d, par, i):
                n = b * (5 * ND) + d * 5
                if i == 0:
                    dve.wait_ge(sp, b * (4 * ND) + d * 4 + 4)
                    nc.vector.tensor_scalar(v[:], sp_e[:], 1.0, -1.0, ALU.add, ALU.add).then_inc(sq, 1)
                elif i == 1:
                    dve.wait_ge(sq, n + 1)
                    nc.vector.scalar_tensor_tensor(v[:], v[:], -1.0, sp_e[:], ALU.mult, ALU.add).then_inc(sq, 1)
                elif i == 2:
                    nc.vector.scalar_tensor_tensor(sp_s[:], sp_s[:], -1.0, sp_e[:], ALU.mult,
                                                   ALU.add).then_inc(sq, 1)
                elif i == 3:
                    dve.wait_ge(sq, n + 2)
                    nc.vector.scalar_tensor_tensor(v[:], sp_l[:], -LN_SLACK, v[:], ALU.add, ALU.add).then_inc(sq, 1)
                elif i == 4:
                    dve.wait_ge(sq, n + 4)
                    nc.vector.tensor_tensor(sp_s[:], sp_s[:], v[:], ALU.max).then_inc(sq, 1)
                else:
                    dve.wait_ge(sq, n + 5)
                    nc.vector.scalar_tensor_tensor(delta[par][:], ps[:, DT_BANK, :], 0.0, sp_s[:], ALU.max,
                                                   ALU.add).then_inc(delta_ready, 1)

            def take_y(b, d, par):
                dve.wait_ge(summed, b * (ND * NP) + d * NP + NP + NP)
                nc.vector.scalar_tensor_tensor(u[:, d, :], u[:, d, :], dsk[:, bass.ds(d, 1)], ps[:, 4 + par, :],
                                               ALU.mult, ALU.add).then_inc(y_taken, 1)

            def step(b, d, par, p, nxt=True, more=True):
                ahead = (d, par, p + LEAD) if p + LEAD < NP else (d + 1, 1 - par, p + LEAD - NP)
                run = p + LEAD < NP or nxt
                if run:
                    scan(b, *ahead[:2], 2 * ahead[2])
                fold(b, d, p)
                if p == 3 and more:
                    softplus(b, d + 2, par, 0)
                    softplus(b, d + 2, par, 1)
                if run:
                    scan(b, *ahead[:2], 2 * ahead[2] + 1)
                if p == 3 and more:
                    softplus(b, d + 2, par, 2)
                    softplus(b, d + 2, par, 3)
                if run:
                    times_c(b, ahead[0], ahead[2])

            def channel_block(b, d, par, nxt=True, more=True):
                for p in range(1, NP):
                    step(b, d, par, p, nxt, more)
                if nxt:
                    step(b, d + 1, 1 - par, 0)
                if more:
                    softplus(b, d + 2, par, 4)
                    softplus(b, d + 2, par, 5)
                take_y(b, d, par)

            with dve.Fori(0, NB) as b:
                for j in range(ND):
                    for c in range(TAPS - 1):
                        lag = c + 1
                        if c == 0:
                            dve.wait_ge(tap_last, b * ND + j + 1)
                        else:
                            dve.wait_ge(taps, b * (ND * (TAPS - 1)) + j * (TAPS - 1) + c)
                        nc.vector.scalar_tensor_tensor(u[:, j, lag:], ps[:, j % 4, 0:T - lag],
                                                       wcv[:, j, TAPS - 1 - lag:TAPS - lag], u[:, j, lag:],
                                                       ALU.mult, ALU.add).then_inc(taps, 1)
                dve.wait_ge(bt_proj, b + 1)
                nc.vector.tensor_copy(b_col[:], ps[:, BT_BANK, :].rearrange("p (a c) -> p a c", a=TT)[:, :, 0:NS]
                                      ).then_inc(bcol_ready, 1)
                for i in range(6):
                    softplus(b, 0, 0, i)
                dve.wait_ge(bcol_ready, b + 1)
                for tb in (0, 1):
                    nc.vector.tensor_tensor(diag_b[:, tb], ident[:].unsqueeze(1).broadcast_to([P, NS, P]),
                                            b_col[:, tb, :].unsqueeze(2).broadcast_to([P, NS, P]),
                                            ALU.mult).then_inc(diag_dve, 1)
                for i in range(6):
                    softplus(b, 1, 1, i)
                for p in range(LEAD):
                    scan(b, 0, 0, 2 * p)
                    scan(b, 0, 0, 2 * p + 1)
                    times_c(b, 0, p)
                step(b, 0, 0, 0)
                with dve.Fori(0, ND // 2 - 1) as j:
                    for par in range(2):
                        channel_block(b, j * 2 + par, par)
                channel_block(b, ND - 2, 0, more=False)
                channel_block(b, ND - 1, 1, nxt=False, more=False)
                dve.wait_ge(x_loaded, b * (16 * TT) + 16 * TT)
                for tb in range(TT):
                    dve.wait_ge(o_proj, b * TT + tb + 1)
                    nc.vector.tensor_tensor(ring[:, tb, 0, :], ps[:, 6 + tb % 2, :], ring[:, tb, 0, :],
                                            ALU.add).then_inc(z_done, 1)
                    dve.wait_ge(z_done, b * TT + tb + 1)
                    nc.vector.bn_stats(st6[:, tb, :], ring[:, tb, 0, :]).then_inc(stats, 1)
                    dve.wait_ge(stats, b * (2 * TT) + 2 * tb + 1)
                    nc.vector.tensor_copy(tick[:], eps[:])
                    nc.vector.bn_aggr(mv[:, tb, :], st6[:, tb, :]).then_inc(stats, 1)
                dve.wait_ge(rstd_ready, b + 1)
                for tb in range(TT):
                    nc.vector.tensor_scalar(ring[:, tb, 0, :], ring[:, tb, 0, :], mv[:, tb, 0:1], rstd[:, tb:tb + 1],
                                            ALU.subtract, ALU.mult).then_inc(normed, 1)

        @block.gpsimd
        def _(pool):
            pool.wait_ge(w_loaded, 16 * N_W)

            def load_wdt(b, d, par):
                nc.gpsimd.tensor_copy(wdt_s[par][:], wdt[:, bass.ts(d, P)]).then_inc(wdt_ready, 1)

            def make_v(b, d, par):
                pool.wait_ge(delta_ready, b * ND + d + 1)
                nc.gpsimd.tensor_tensor(v[:], delta[par][:], u[:, d, :], ALU.mult).then_inc(v_ready, 1)

            def times_c(b, d, p):
                k = 2 * p
                if p == 0 and isinstance(d, int) and d == 0:
                    pool.wait_ge(c_loaded, b * 16 + 16)
                pool.wait_ge(scanned, b * (ND * NU) + d * NU + k + 3)
                nc.gpsimd.tensor_tensor(ring[:, k], ring[:, k], c_row[:, 2 * k:2 * k + 2, :],
                                        ALU.mult).then_inc(c_pool, 1)

            def add_pair(b, d, p):
                k = 2 * p
                pool.wait_ge(c_pool, b * (ND * NP) + d * NP + p + 1)
                pool.wait_ge(c_dve, b * (ND * NP) + d * NP + p + 1)
                nc.gpsimd.tensor_tensor(ring[:, k], ring[:, k], ring[:, k + 1], ALU.add).then_inc(paired, 1)

            def gate_y(b, d):
                pool.wait_ge(y_taken, b * ND + d + 3)
                nc.gpsimd.tensor_tensor(gate[:, d, :], gate[:, d, :], u[:, d, :], ALU.mult).then_inc(yg_ready, 1)

            def step(b, d, par, p, nxt=True, more=True):
                if p + 1 < NP:
                    add_pair(b, d, p + 1)
                elif nxt:
                    add_pair(b, d + 1, 0)
                if p + LEAD < NP:
                    times_c(b, d, p + LEAD)
                elif nxt:
                    times_c(b, d + 1, p + LEAD - NP)
                if p == 1 and more:
                    load_wdt(b, d + 2, par)

            def channel_block(b, d, par, nxt=True, more=True):
                if nxt:
                    make_v(b, d + 1, 1 - par)
                for p in range(1, NP):
                    step(b, d, par, p, nxt, more)
                if nxt:
                    step(b, d + 1, 1 - par, 0)
                gate_y(b, d)

            with pool.Fori(0, NB) as b:
                load_wdt(b, 0, 0)
                load_wdt(b, 1, 1)
                pool.wait_ge(bcol_ready, b + 1)
                for tb in (2, 3):
                    nc.gpsimd.tensor_tensor(diag_b[:, tb], ident[:].unsqueeze(1).broadcast_to([P, NS, P]),
                                            b_col[:, tb, :].unsqueeze(2).broadcast_to([P, NS, P]),
                                            ALU.mult).then_inc(diag_pool, 1)
                    if tb == 2:
                        make_v(b, 0, 0)
                times_c(b, 0, 0)
                add_pair(b, 0, 0)
                times_c(b, 0, 1)
                step(b, 0, 0, 0)
                with pool.Fori(0, ND // 2 - 1) as j:
                    for par in range(2):
                        channel_block(b, j * 2 + par, par)
                channel_block(b, ND - 2, 0, more=False)
                channel_block(b, ND - 1, 1, nxt=False, more=False)


def cross_attention_ffn_pass(nc, x1, ctx_t, attn_mask, pad_mask, wq, wk, wv, wo, bq, bk, bv, bo,
                             wr, wkf, wvf, mu_r, mu_k, ident_d, out):
    NB, T, DM = x1.shape
    NK = ctx_t.shape[2] // NB
    KT = DM // P
    TT = T // P
    DK = 32
    NH = DM // DK
    HB = P // DK
    HW = HB * NK
    SCALE = 1.0 / DK ** 0.5
    MASKED = -3e38
    LIVE = -1e38
    KB = 4
    SETUP_A, SETUP_V = KT * (NB // KB), NB
    FRONT, FFN, ATTEND = 2 * KT, 3 * KT, NH + KT
    ROW_A = FRONT + FFN + ATTEND
    ROW_V = TT * KT + TT + TT

    def front_a(b):
        return SETUP_A if isinstance(b, int) and b == 0 else b * ROW_A + (SETUP_A - FFN)

    def attend_a(b):
        return b * ROW_A + (SETUP_A + FRONT)

    def scores_v(b):
        return SETUP_V if isinstance(b, int) and b == 0 else b * ROW_V + (SETUP_V - TT)

    def out_v(b):
        return b * ROW_V + (SETUP_V + TT * KT)

    LAST_A, LAST_V = attend_a(NB - 1) + ATTEND, out_v(NB - 1) + TT

    ctx = ExitStack()
    with ctx:
        def sb(name, shape, dt=FP32):
            return ctx.enter_context(nc.sbuf_tensor("xf_" + name, shape, dt))

        def sem(name):
            return ctx.enter_context(nc.semaphore("xf_" + name))

        def wait_at_least(eng, s, value):
            if not (isinstance(value, int) and value <= 0):
                eng.wait_ge(s, value)

        wq_s, wo_s, wr_s, wkf_s, wvf_s = (sb(n, [P, KT, DM]) for n in ("wq", "wo", "wr", "wkf", "wvf"))
        kbd = sb("kbd", [P, NB, KT, HW])
        v_all = sb("v_all", [P, NB, DM])
        v_cur = sb("v_cur", [P, DM])
        xn = [sb(f"xn{i}", [P, TT, DM]) for i in range(2)]
        x1t = sb("x1t", [P, KT, T])
        ot = x1t
        qt = sb("qt", [P, KT, T])
        kf = qt
        pr = sb("pr", [P, TT, NH, NK])
        pt = sb("pt", [P, 2 * HB, T])
        x2t = sb("x2t", [P, KT, T + 1])
        xr, xk = sb("xr", [P, KT, T]), sb("xk", [P, KT, T])
        r_s = sb("r_s", [P, TT, DM])
        ctx_s = pt[:].rearrange("p a t -> p (a t)")[:, 0:KT * NB * NK].rearrange("p (k n) -> p k n", k=KT)
        wk_s, wv_s, bv_s = xr, xk, r_s[:, 0, :]
        bo_s = sb("bo_s", [P, DM])
        bq_s, bk_s, mur, muk, omr, omk = (sb(n, [P, KT]) for n in ("bq", "bk", "mur", "muk", "omr", "omk"))
        am_u, pm_u = sb("am_u", [P, TT, NK], U8), sb("pm_u", [P, NB, NK], U8)
        am, pm = sb("am", [P, TT, NK]), sb("pm", [P, NB, NK])
        mask = sb("mask", [P, TT, NK])
        ident = sb("ident", [P, P])
        eps = sb("eps", [P, 1])
        tick = sb("tick", [P, 1])
        top, total, live = (sb(n, [P, TT, NH]) for n in ("top", "total", "live"))
        st6, mv, rstd = sb("st6", [P, TT, 6]), sb("mv", [P, TT, 2]), sb("rstd", [P, TT])
        gst6, gmv, grstd = sb("gst6", [P, TT, 6]), sb("gmv", [P, TT, 2]), sb("grstd", [P, TT])

        ps = ctx.enter_context(nc.psum_tensor("xf_ps", [P, 8, T], FP32))

        w_loaded = sem("w_loaded")
        x_loaded = sem("x_loaded")
        zeroed = sem("zeroed")
        consts = sem("consts")
        a_filled, a_taken = sem("a_filled"), sem("a_taken")
        v_filled, v_taken = sem("v_filled"), sem("v_taken")
        biased = sem("biased")
        v_here = sem("v_here")
        masked = sem("masked")
        topped = sem("topped")
        centred = sem("centred")
        exped = sem("exped")
        shares = sem("shares")
        probs = sem("probs")
        mixed = sem("mixed")
        squared = sem("squared")
        z2_stats = sem("z2_stats")
        rstd2_ln, rstd2 = sem("rstd2_ln"), sem("rstd2")
        normed2 = sem("normed2")
        z3 = sem("z3")
        z3_stats = sem("z3_stats")
        rstd3_ln, rstd3 = sem("rstd3_ln"), sem("rstd3")
        normed3 = sem("normed3")
        stored = sem("stored")

        block = ctx.enter_context(nc.Block())

        def rows(body, eng):
            body(0, 0)
            with eng.Fori(0, (NB - 2) // 2) as i:
                for s in range(2):
                    body(i * 2 + (1 + s), 1 - s)
            body(NB - 1, (NB - 1) % 2)

        loads = [(wk_s[:], wk), (ctx_s, ctx_t), (bk_s[:], bk), (wv_s[:], wv),
                 (bv_s, bv.unsqueeze(0).broadcast_to([P, DM])), (ident[:], ident_d), (wq_s[:], wq), (bq_s[:], bq),
                 (am_u[:], attn_mask), (pm_u[:], pad_mask.unsqueeze(0).broadcast_to([P, NB, NK])),
                 (bo_s[:], bo.unsqueeze(0).broadcast_to([P, DM])), (wo_s[:], wo), (mur[:], mu_r), (muk[:], mu_k),
                 (wr_s[:], wr), (wkf_s[:], wkf), (wvf_s[:], wvf)]

        @block.sync
        def _(sp):
            def load(b, par):
                for tb in range(TT):
                    sp.dma_start(xn[par][:, tb, :], x1[b, tb * P:(tb + 1) * P, :]).then_inc(x_loaded, 16)

            def store(b, par):
                for tb in range(TT):
                    sp.wait_ge(normed3, b * TT + tb + 1)
                    sp.dma_start(out[b, tb * P:(tb + 1) * P, :], xn[par][:, tb, :]).then_inc(stored, 16)

            for dst, src in loads[:6]:
                sp.dma_start(dst, src).then_inc(w_loaded, 16)
            load(0, 0)
            for dst, src in loads[6:]:
                sp.dma_start(dst, src).then_inc(w_loaded, 16)

            def row(b, par):
                if isinstance(b, int) and b == 0:
                    load(1, 1)
                    return
                store(b - 1, 1 - par)
                if not (isinstance(b, int) and b == NB - 1):
                    sp.wait_ge(stored, b * (16 * TT))
                    load(b + 1, 1 - par)

            rows(row, sp)
            store(NB - 1, (NB - 1) % 2)
            sp.wait_ge(stored, NB * TT * 16)

        @block.tensor
        def _(pe):
            pe.wait_ge(w_loaded, 16 * len(loads))

            def a_bank(a):
                wait_at_least(pe, a_taken, a - 4)

            def v_bank(v):
                wait_at_least(pe, v_taken, v - 4)

            def product_a(a, i, lhs_t, rhs):
                a_bank(a + (i + 1))
                for kt in range(KT):
                    m = nc.tensor.matmul(ps[:, i % 4, :], lhs_t(kt), rhs(kt), start=(kt == 0), stop=(kt == KT - 1))
                m.then_inc(a_filled, 1)

            def product_v(v, i, lhs_t, rhs):
                v_bank(v + (i + 1))
                for kt in range(KT):
                    m = nc.tensor.matmul(ps[:, 4 + i % 4, :], lhs_t(kt), rhs(kt), start=(kt == 0), stop=(kt == KT - 1))
                m.then_inc(v_filled, 1)

            def transposed(a, i, source):
                a_bank(a + (i + 1))
                for tb in range(TT):
                    m = nc.tensor.transpose(ps[:, i % 4, tb * P:(tb + 1) * P], source[:, tb, i * P:(i + 1) * P],
                                            ident[:])
                m.then_inc(a_filled, 1)

            def front(b, par):
                a = front_a(b)
                pe.wait_ge(x_loaded, b * (16 * TT) + 16 * TT)
                for kt in range(KT):
                    transposed(a, kt, xn[par])
                pe.wait_ge(a_taken, a + KT)
                for j in range(KT):
                    product_a(a, KT + j, lambda kt: wq_s[:, kt, j * P:(j + 1) * P], lambda kt: x1t[:, kt, :])

            def x2_transposes(b, a, par):
                pe.wait_ge(normed2, b * TT + TT)
                for kt in range(KT):
                    transposed(a, kt, xn[par])

            def scores(b):
                v = scores_v(b)
                pe.wait_ge(a_taken, front_a(b) + 2 * KT)
                for tb in range(TT):
                    for j in range(KT):
                        v_bank(v + (tb * KT + j + 1))
                        nc.tensor.matmul(ps[:, 4 + j, 0:HW], qt[:, j, tb * P:(tb + 1) * P], kbd[:, b, j, :],
                                         start=True, stop=True).then_inc(v_filled, 1)

            def ffn(b, a, v):
                for tb in range(TT):
                    pe.wait_ge(mixed, b * (2 * KT) + 2 * KT)
                    product_a(a, KT + tb, lambda kt: xr[:, kt, tb * P:(tb + 1) * P], lambda kt: wr_s[:, kt, :])
                for j in range(KT):
                    product_a(a, 2 * KT + j, lambda kt: wkf_s[:, kt, j * P:(j + 1) * P], lambda kt: xk[:, kt, :])
                pe.wait_ge(squared, b * KT + KT)
                for tb in range(TT):
                    product_v(v, tb, lambda kt: kf[:, kt, tb * P:(tb + 1) * P], lambda kt: wvf_s[:, kt, :])

            def attend(b):
                a, v = attend_a(b), out_v(b)
                n = 0

                def values(j, n):
                    pe.wait_ge(a_taken, a + ends[j])
                    a_bank(a + (n + 1))
                    for i in range(HB):
                        h = j * HB + i
                        m = nc.tensor.matmul(ps[i * DK:(i + 1) * DK, n % 4, :], v_cur[0:NK, h * DK:(h + 1) * DK],
                                             pt[0:NK, h % (2 * HB), :], start=True, stop=True,
                                             tile_position=(0, i * DK))
                    m.then_inc(a_filled, 1)

                pe.wait_ge(probs, b * TT + TT)
                pe.wait_ge(v_here, b + 1)
                ends = []
                for j in range(KT):
                    for i in range(HB):
                        h = j * HB + i
                        a_bank(a + (n + 1))
                        for tb in range(TT):
                            m = nc.tensor.transpose(ps[0:NK, n % 4, tb * P:(tb + 1) * P], pr[:, tb, h, :], ident[:])
                        m.then_inc(a_filled, 1)
                        n += 1
                    ends.append(n)
                    if j >= 1:
                        values(j - 1, n)
                        n += 1
                values(KT - 1, n)
                pe.wait_ge(a_taken, a + ATTEND)
                for tb in range(TT):
                    product_v(v, tb, lambda kt: ot[:, kt, tb * P:(tb + 1) * P], lambda kt: wo_s[:, kt, :])

            for half in range(NB // KB):
                for j in range(KT):
                    i = half * KT + j
                    a_bank(i + 1)
                    for kt in range(KT):
                        m = nc.tensor.matmul(ps[:, j, 0:KB * NK], wk_s[:, kt, j * P:(j + 1) * P],
                                             ctx_s[:, kt, half * KB * NK:(half + 1) * KB * NK],
                                             start=(kt == 0), stop=(kt == KT - 1))
                    m.then_inc(a_filled, 1)
            for i in range(NB):
                v_bank(i + 1)
                for kt in range(KT):
                    m = nc.tensor.matmul(ps[0:NK, 4 + i % 4, :], ctx_s[:, kt, i * NK:(i + 1) * NK], wv_s[:, kt, :],
                                         start=(kt == 0), stop=(kt == KT - 1))
                m.then_inc(v_filled, 1)

            def row(b, par):
                first = isinstance(b, int) and b == 0
                front(b, par)
                if not first:
                    x2_transposes(b - 1, front_a(b) + FRONT, 1 - par)
                scores(b)
                if not first:
                    ffn(b - 1, front_a(b) + FRONT, scores_v(b) + TT * KT)
                attend(b)

            rows(row, pe)
            x2_transposes(NB - 1, LAST_A, (NB - 1) % 2)
            ffn(NB - 1, LAST_A, LAST_V)

        @block.scalar
        def _(act):
            act.wait_ge(w_loaded, 16 * len(loads))
            act.wait_ge(zeroed, 2)
            act.wait_ge(consts, 5)
            for half in range(NB // KB):
                for j in range(KT):
                    act.wait_ge(a_filled, half * KT + j + 1)
                    for i in range(HB):
                        r0 = i * DK
                        s = nc.scalar.activation(
                            kbd[r0:r0 + DK, half * KB:(half + 1) * KB, j, i * NK:(i + 1) * NK],
                            ps[r0:r0 + DK, j, 0:KB * NK].rearrange("p (b n) -> p b n", b=KB),
                            ACT.Identity, bias=bk_s[r0:r0 + DK, j:j + 1])
                    s.then_inc(a_taken, 1)

            def front_x(b):
                a = front_a(b)
                for kt in range(KT):
                    act.wait_ge(a_filled, a + (kt + 1))
                    nc.scalar.copy(x1t[:, kt, :], ps[:, kt, :]).then_inc(a_taken, 1)

            def front_q(b):
                a = front_a(b)
                for j in range(KT):
                    act.wait_ge(a_filled, a + (KT + j + 1))
                    nc.scalar.activation(qt[:, j, :], ps[:, j, :], ACT.Identity,
                                         bias=bq_s[:, j:j + 1]).then_inc(a_taken, 1)

            def rstd_of(stats, n, var, dst, ln_done, done, b):
                act.wait_ge(stats, b * n + n)
                nc.scalar.activation(dst[:], var[:, :, 1], ACT.Ln, bias=eps[:]).then_inc(ln_done, 1)
                act.wait_ge(ln_done, b + 1)
                nc.scalar.activation(dst[:], dst[:], ACT.Exp, scale=-0.5).then_inc(done, 1)

            def take_x2(b, a):
                for kt in range(KT):
                    act.wait_ge(a_filled, a + (kt + 1))
                    nc.scalar.activation(xr[:, kt, :], ps[:, kt, :], ACT.Copy, scale=mur[:, kt:kt + 1])
                    nc.scalar.activation(xk[:, kt, :], ps[:, kt, :], ACT.Copy, scale=muk[:, kt:kt + 1])
                    nc.scalar.copy(x2t[:, kt, 1:], ps[:, kt, :]).then_inc(a_taken, 1)

            def exps(b):
                for tb in range(TT):
                    act.wait_ge(centred, b * TT + tb + 1)
                    nc.scalar.activation(pr[:, tb], pr[:, tb], ACT.Exp).then_inc(exped, 1)

            def ffn(b, a):
                for tb in range(TT):
                    act.wait_ge(a_filled, a + (KT + tb + 1))
                    nc.scalar.activation(r_s[:, tb, :], ps[:, tb, :], ACT.Sigmoid).then_inc(a_taken, 1)
                for j in range(KT):
                    act.wait_ge(a_filled, a + (2 * KT + j + 1))
                    nc.scalar.activation(kf[:, j, :], ps[:, j, :], ACT.Relu).then_inc(a_taken, 1)

            def rstd_ffn(b):
                rstd_of(z3_stats, 2 * TT, gmv, grstd, rstd3_ln, rstd3, b)

            def attend(b, before):
                a = attend_a(b)
                n = 0

                def values(j, n):
                    act.wait_ge(a_filled, a + (n + 1))
                    nc.scalar.copy(ot[:, j, :], ps[:, n % 4, :]).then_inc(a_taken, 1)

                for j in range(KT):
                    for i in range(HB):
                        h = j * HB + i
                        act.wait_ge(a_filled, a + (n + 1))
                        nc.scalar.copy(pt[0:NK, h % (2 * HB), :], ps[0:NK, n % 4, :]).then_inc(a_taken, 1)
                        n += 1
                    if j >= 1:
                        values(j - 1, n)
                        n += 1
                    if j == 1 and before:
                        rstd_ffn(b - 1)
                values(KT - 1, n)

            def row(b, par):
                first = isinstance(b, int) and b == 0
                front_x(b)
                if not first:
                    rstd_of(z2_stats, 2 * TT, mv, rstd, rstd2_ln, rstd2, b - 1)
                front_q(b)
                if not first:
                    take_x2(b - 1, front_a(b) + FRONT)
                exps(b)
                if not first:
                    ffn(b - 1, front_a(b) + FRONT)
                attend(b, not first)

            rows(row, act)
            rstd_of(z2_stats, 2 * TT, mv, rstd, rstd2_ln, rstd2, NB - 1)
            take_x2(NB - 1, LAST_A)
            ffn(NB - 1, LAST_A)
            rstd_ffn(NB - 1)

        @block.vector
        def _(dve):
            dve.wait_ge(w_loaded, 16 * len(loads))
            nc.vector.tensor_scalar(am[:], am_u[:], MASKED, None, ALU.mult).then_inc(consts, 1)
            nc.vector.tensor_scalar(pm[:], pm_u[:], MASKED, None, ALU.mult).then_inc(consts, 1)
            nc.vector.tensor_scalar(omr[:], mur[:], -1.0, 1.0, ALU.mult, ALU.add).then_inc(consts, 1)
            nc.vector.tensor_scalar(omk[:], muk[:], -1.0, 1.0, ALU.mult, ALU.add).then_inc(consts, 1)
            nc.vector.memset(eps[:], EPS).then_inc(consts, 1)
            for i in range(NB):
                dve.wait_ge(v_filled, i + 1)
                nc.vector.tensor_tensor(v_all[0:NK, i, :], ps[0:NK, 4 + i % 4, :], bv_s[0:NK, :],
                                        ALU.add).then_inc(v_taken, 1)
            dve.wait_ge(consts, 5)
            dve.wait_ge(zeroed, 2)

            def shares_of(b, tb):
                n = (b * TT + tb) * 4
                dve.wait_ge(exped, b * TT + tb + 1)
                nc.vector.tensor_reduce(total[:, tb], pr[:, tb], AX.X, ALU.add).then_inc(shares, 1)
                nc.vector.tensor_scalar(live[:, tb], top[:, tb], LIVE, None, ALU.is_gt).then_inc(shares, 1)
                dve.wait_ge(shares, n + 2)
                nc.vector.tensor_tensor(total[:, tb], total[:, tb], live[:, tb], ALU.mult).then_inc(shares, 1)
                dve.wait_ge(shares, n + 3)
                nc.vector.reciprocal(total[:, tb], total[:, tb]).then_inc(shares, 1)

            def softmax(b):
                v = scores_v(b)
                nc.vector.tensor_tensor(mask[:], am[:], pm[:, bass.ds(b, 1), :].broadcast_to([P, TT, NK]),
                                        ALU.min).then_inc(masked, 1)
                dve.wait_ge(masked, b + 1)
                for tb in range(TT):
                    for j in range(KT):
                        dve.wait_ge(v_filled, v + (tb * KT + j + 1))
                        nc.vector.scalar_tensor_tensor(
                            pr[:, tb, j * HB:(j + 1) * HB, :],
                            ps[:, 4 + j, 0:HW].rearrange("p (h n) -> p h n", h=HB), SCALE,
                            mask[:, tb, :].unsqueeze(1).broadcast_to([P, HB, NK]),
                            ALU.mult, ALU.add).then_inc(v_taken, 1)
                    dve.wait_ge(v_taken, v + (tb + 1) * KT)
                    nc.vector.tensor_reduce(top[:, tb], pr[:, tb], AX.X, ALU.max).then_inc(topped, 1)
                    if tb >= 1:
                        dve.wait_ge(topped, b * TT + tb)
                        shares_of(b, tb - 1)
                dve.wait_ge(topped, b * TT + TT)
                shares_of(b, TT - 1)

            def norms(b, par, stats_mv, rs, ready, done):
                dve.wait_ge(ready, b + 1)
                for tb in range(TT):
                    nc.vector.tensor_scalar(xn[par][:, tb, :], xn[par][:, tb, :], stats_mv[:, tb, 0:1],
                                            rs[:, tb:tb + 1], ALU.subtract, ALU.mult).then_inc(done, 1)

            def mixes(b, a):
                for kt in range(KT):
                    dve.wait_ge(a_taken, a + (kt + 1))
                    for dst, om in ((xr, omr), (xk, omk)):
                        nc.vector.scalar_tensor_tensor(dst[:, kt, :], x2t[:, kt, 0:T], om[:, kt:kt + 1], dst[:, kt, :],
                                                       ALU.mult, ALU.add).then_inc(mixed, 1)

            def ffn_out(b, v, par):
                for tb in range(TT):
                    dve.wait_ge(v_filled, v + (tb + 1))
                    nc.vector.tensor_tensor(r_s[:, tb, :], r_s[:, tb, :], ps[:, 4 + tb, :], ALU.mult
                                            ).then_inc(v_taken, 1)
                    dve.wait_ge(v_taken, v + (tb + 1))
                    nc.vector.tensor_tensor(xn[par][:, tb, :], xn[par][:, tb, :], r_s[:, tb, :],
                                            ALU.add).then_inc(z3, 1)
                    dve.wait_ge(z3, b * TT + tb + 1)
                    nc.vector.bn_stats(gst6[:, tb, :], xn[par][:, tb, :]).then_inc(z3_stats, 1)
                    dve.wait_ge(z3_stats, b * (2 * TT) + 2 * tb + 1)
                    nc.vector.tensor_copy(tick[:], eps[:])
                    nc.vector.bn_aggr(gmv[:, tb, :], gst6[:, tb, :]).then_inc(z3_stats, 1)

            def attention_out(b, par):
                v = out_v(b)
                for tb in range(TT):
                    dve.wait_ge(v_filled, v + (tb + 1))
                    if tb == 0:
                        dve.wait_ge(biased, b * TT + TT)
                    nc.vector.tensor_tensor(xn[par][:, tb, :], xn[par][:, tb, :], ps[:, 4 + tb, :],
                                            ALU.add).then_inc(v_taken, 1)
                    dve.wait_ge(v_taken, v + (tb + 1))
                    nc.vector.bn_stats(st6[:, tb, :], xn[par][:, tb, :]).then_inc(z2_stats, 1)
                    dve.wait_ge(z2_stats, b * (2 * TT) + 2 * tb + 1)
                    nc.vector.tensor_copy(tick[:], eps[:])
                    nc.vector.bn_aggr(mv[:, tb, :], st6[:, tb, :]).then_inc(z2_stats, 1)

            def row(b, par):
                first = isinstance(b, int) and b == 0
                if not first:
                    norms(b - 1, 1 - par, mv, rstd, rstd2, normed2)
                    mixes(b - 1, front_a(b) + FRONT)
                softmax(b)
                if not first:
                    ffn_out(b - 1, scores_v(b) + TT * KT, 1 - par)
                    norms(b - 1, 1 - par, gmv, grstd, rstd3, normed3)
                attention_out(b, par)

            rows(row, dve)
            last = (NB - 1) % 2
            norms(NB - 1, last, mv, rstd, rstd2, normed2)
            mixes(NB - 1, LAST_A)
            ffn_out(NB - 1, LAST_V, last)
            norms(NB - 1, last, gmv, grstd, rstd3, normed3)

        @block.gpsimd
        def _(pool):
            nc.gpsimd.memset(kbd[:], 0.0).then_inc(zeroed, 1)
            nc.gpsimd.memset(x2t[:, :, 0:1], 0.0).then_inc(zeroed, 1)
            pool.wait_ge(w_loaded, 16 * len(loads))
            pool.wait_ge(v_taken, NB)

            def prepare(b, par):
                pool.wait_ge(a_filled, front_a(b) + KT)
                for tb in range(TT):
                    nc.gpsimd.tensor_tensor(xn[par][:, tb, :], xn[par][:, tb, :], bo_s[:], ALU.add).then_inc(biased, 1)
                nc.gpsimd.tensor_copy(v_cur[0:NK, :], v_all[0:NK, b, :]).then_inc(v_here, 1)

            def softmax(b):
                def centre(tb):
                    pool.wait_ge(topped, b * TT + tb + 1)
                    nc.gpsimd.tensor_tensor(pr[:, tb], pr[:, tb], top[:, tb].unsqueeze(2).broadcast_to([P, NH, NK]),
                                            ALU.subtract).then_inc(centred, 1)

                def weigh(tb):
                    pool.wait_ge(shares, (b * TT + tb) * 4 + 4)
                    nc.gpsimd.tensor_tensor(pr[:, tb], pr[:, tb], total[:, tb].unsqueeze(2).broadcast_to([P, NH, NK]),
                                            ALU.mult).then_inc(probs, 1)

                for tb in range(TT):
                    centre(tb)
                    if tb >= 1:
                        weigh(tb - 1)
                weigh(TT - 1)

            def squares(b, a):
                for j in range(KT):
                    pool.wait_ge(a_taken, a + (2 * KT + j + 1))
                    nc.gpsimd.tensor_tensor(kf[:, j, :], kf[:, j, :], kf[:, j, :], ALU.mult).then_inc(squared, 1)

            def row(b, par):
                first = isinstance(b, int) and b == 0
                prepare(b, par)
                softmax(b)
                if not first:
                    squares(b - 1, front_a(b) + FRONT)

            rows(row, pool)
            squares(NB - 1, LAST_A)


def decoder_layer(nc, t, out):
    x = t["x"]
    ns = t["a_log"].shape[2]
    c_dram = nc.dram_tensor("c_rows", (ns, x.shape[1]), FP32).ap()
    x1 = nc.dram_tensor("x1", x.shape, FP32).ap()
    mamba_pass(nc, x, t["x_t"], c_dram, t["w_in"], t["w_conv"], t["b_conv"], t["w_x"], t["w_dt"], t["a_log"],
               t["d_skip"], t["w_out"], t["ident"], x1)
    cross_attention_ffn_pass(nc, x1, t["ctx_t"], t["attn_mask"], t["pad_mask"], t["wq"], t["wk"], t["wv"], t["wo"],
                             t["bq"], t["bk"], t["bv"], t["bo"], t["wr"], t["wkf"], t["wvf"], t["mu_r"], t["mu_k"],
                             t["ident"], out)




def kernel(**inputs):
    import numpy as np
    import concourse.bacc as bacc
    from concourse.bass_utils import run_bass_kernel_spmd

    a = {k: np.asarray(v) for k, v in inputs.items()}

    def blocks(w, p=P):
        return np.ascontiguousarray(w.reshape(w.shape[0] // p, p, -1).transpose(1, 0, 2))

    di, dtr = a["L0_attn_W_dt"].shape
    ns = a["L0_attn_A_log"].shape[1]
    wxp = a["L0_attn_W_xproj"].T
    w_x = np.zeros((di, P), np.float32)
    w_x[:, :dtr] = wxp[:, :dtr]
    w_x[:, dtr + 1:dtr + 1 + 2 * ns] = wxp[:, dtr:]
    w_dt = np.zeros((P, di), np.float32)
    w_dt[:dtr] = a["L0_attn_W_dt"].T
    w_dt[dtr] = a["L0_attn_b_dt"]
    arrays = {
        "x": a["x"],
        "x_t": np.ascontiguousarray(a["x"].reshape(a["x"].shape[0], a["x"].shape[1], -1, P).transpose(0, 3, 2, 1)),
        "w_in": blocks(a["L0_attn_W_in"].T),
        "w_conv": blocks(a["L0_attn_W_conv"].reshape(di, -1)),
        "b_conv": np.ascontiguousarray(a["L0_attn_b_conv"].reshape(-1, P).T),
        "w_x": blocks(w_x),
        "w_dt": w_dt,
        "a_log": blocks(a["L0_attn_A_log"]),
        "d_skip": np.ascontiguousarray(a["L0_attn_D"].reshape(-1, P).T),
        "w_out": blocks(a["L0_attn_W_out"].T),
        "ident": np.eye(P, dtype=np.float32),
    }
    column = lambda v: np.ascontiguousarray(v.reshape(-1, P).T)
    arrays.update({
        "ctx_t": blocks(a["ctx_1024"].reshape(-1, a["ctx_1024"].shape[2]).T),
        "attn_mask": blocks(a["mask_SxS2_bk1"]),
        "pad_mask": a["mask_BxS2_bf0"],
        "bv": a["L0_xattn_bv"], "bo": a["L0_xattn_bo"],
        "bq": column(a["L0_xattn_bq"]), "bk": column(a["L0_xattn_bk"]),
        "mu_r": column(a["L0_ffn_mu_r"]), "mu_k": column(a["L0_ffn_mu_k"]),
        "wq": blocks(a["L0_xattn_Wq"].T), "wk": blocks(a["L0_xattn_Wk"].T), "wv": blocks(a["L0_xattn_Wv"].T),
        "wo": blocks(a["L0_xattn_Wo"].T), "wr": blocks(a["L0_ffn_W_r"].T), "wkf": blocks(a["L0_ffn_W_k"].T),
        "wvf": blocks(a["L0_ffn_W_v"].T),
    })
    nc = bacc.Bacc("TRN2", target_bir_lowering=False, num_devices=1)
    t = {n: nc.dram_tensor(n, v.shape, mybir.dt.from_np(v.dtype), kind="ExternalInput").ap()
         for n, v in arrays.items()}
    out = nc.dram_tensor("out", a["x"].shape, FP32, kind="ExternalOutput").ap()
    decoder_layer(nc, t, out)
    r = run_bass_kernel_spmd(nc, [arrays], core_ids=[0])
    return r.results[0]["out"]
```

```python
import concourse.bass as bass
from concourse import mybir
from contextlib import ExitStack

FP32 = mybir.dt.float32
U8 = mybir.dt.uint8
ALU = mybir.AluOpType
ACT = mybir.ActivationFunctionType
AX = mybir.AxisListType

P = 128
EPS = 1e-5


def mamba_pass(nc, x, x_t, c_dram, w_u, w_res, w_conv, b_conv, w_x, w_dt, a_log, d_skip, w_out, ident_d, x1):
    NB, T, DM = x.shape
    DI = w_u.shape[2]
    NS = a_log.shape[2]
    KT = DM // P
    ND = DI // P
    TT = T // P
    TAPS = w_conv.shape[2]
    DTR = 32
    B0, C0 = DTR + 1, DTR + 1 + NS
    NU = NS // 2
    NP = NU // 2
    LEAD = 2
    LN_SLACK = 3e-10

    ctx = ExitStack()
    with ctx:
        def sb(name, shape, dt=FP32):
            return ctx.enter_context(nc.sbuf_tensor("mamba_" + name, shape, dt))

        def sem(name):
            return ctx.enter_context(nc.semaphore(name))

        wu = sb("wu", [P, KT, DI])
        wres_s = [sb(f"wres_s{i}", [P, KT, P]) for i in range(2)]
        wout = sb("wout", [P, ND, DM])
        wx = sb("wx", [P, ND, P])
        wcv = sb("wcv", [P, ND, TAPS])
        bcv = sb("bcv", [P, ND])
        a_neg = sb("a_neg", [P, ND, NS])
        dsk = sb("dsk", [P, ND])
        ident = sb("ident", [P, P])
        eps = sb("eps", [P, 1])
        tick = sb("tick", [P, 1])
        xt = sb("xt", [P, KT, T])
        u = sb("u", [P, ND, T])
        gate = [sb(f"gate{i}", [P, T]) for i in range(2)]
        diag_b = sb("diag_b", [P, TT, NS, P])
        c_row = sb("c_row", [P, NS, T])
        xdbl = sb("xdbl", [P, T])
        b_col = sb("b_col", [P, TT, NS])
        wdt_s = [sb(f"wdt_s{i}", [P, P]) for i in range(2)]
        sp_e = sb("sp_e", [P, T])
        sp_l = sb("sp_l", [P, T])
        sp_s = sb("sp_s", [P, T])
        sp_w = sb("sp_w", [P, T])
        delta = [sb(f"delta{i}", [P, T]) for i in range(2)]
        v = sb("v", [P, T])
        v_t = [sb(f"v_t{i}", [P, T]) for i in range(2)]
        ring = sb("ring", [P, NU, 2, T])
        zero2 = sb("zero2", [P, 2, 1])
        st6 = sb("st6", [P, TT, 6])
        mv = sb("mv", [P, TT, 2])
        rstd = sb("rstd", [P, TT])

        ps = ctx.enter_context(nc.psum_tensor("ps", [P, 8, T], FP32))
        BT_BANK, DT_BANK = 6, 7

        w_loaded = sem("w_loaded")
        w_rest_loaded = sem("w_rest_loaded")
        a_exp = sem("a_exp")
        consts = sem("consts")
        xt_loaded = sem("xt_loaded")
        u_proj = sem("u_proj")
        tap_last = sem("tap_last")
        taps = sem("taps")
        u_ready = sem("u_ready")
        x_proj = sem("x_proj")
        xdbl_ready = sem("xdbl_ready")
        bt_proj = sem("bt_proj")
        bcol_ready = sem("bcol_ready")
        diag_dve = sem("diag_dve")
        diag_pool = sem("diag_pool")
        c_stored = sem("c_stored")
        c_loaded = [sem(f"c_loaded{p}") for p in range(NP)]
        r_proj = sem("r_proj")
        r_taken = sem("r_taken")
        wdt_loaded = [sem(f"wdt_loaded{i}") for i in range(2)]
        wres_loaded = [sem(f"wres_loaded{i}") for i in range(2)]
        dt_proj = sem("dt_proj")
        sp = sem("sp")
        sq = sem("sq")
        delta_ready = sem("delta_ready")
        v_ready = sem("v_ready")
        vt_proj = sem("vt_proj")
        vt_ready = sem("vt_ready")
        da_ready = sem("da_ready")
        dbu_ready = sem("dbu_ready")
        scanned = sem("scanned")
        c_pool = sem("c_pool")
        c_dve = sem("c_dve")
        paired = sem("paired")
        folded = sem("folded")
        summed = sem("summed")
        y_taken = sem("y_taken")
        yg_ready = sem("yg_ready")
        x_loaded = sem("x_loaded")
        o_proj = sem("o_proj")
        z_done = sem("z_done")
        stats = sem("stats")
        rstd_ln = sem("rstd_ln")
        rstd_ready = sem("rstd_ready")
        normed = sem("normed")
        stored = sem("stored")

        loads = [(ident, ident_d), (wcv, w_conv), (bcv, b_conv), (a_neg, a_log), (wu, w_u)]
        rest_loads = [(dsk, d_skip), (wx, w_x), (wout, w_out)]
        block = ctx.enter_context(nc.Block())

        @block.sync
        def _(sp_eng):
            for dst, src in loads:
                sp_eng.dma_start(dst[:], src).then_inc(w_loaded, 16)
            sp_eng.dma_start(xt[:], x_t[0]).then_inc(xt_loaded, 16)
            for dst, src in rest_loads:
                sp_eng.dma_start(dst[:], src).then_inc(w_rest_loaded, 16)

            def load_wdt(d, par):
                sp_eng.dma_start(wdt_s[par][:], w_dt[d]).then_inc(wdt_loaded[par], 16)

            def load_wres(d, par):
                sp_eng.dma_start(wres_s[par][:], w_res[d]).then_inc(wres_loaded[par], 16)

            for d in range(2):
                load_wdt(d, d)
                load_wres(d, d)

            def row(b, last=False):
                sp_eng.wait_ge(xdbl_ready, b + 1)
                sp_eng.dma_start(c_dram, xdbl[C0:C0 + NS, :]).then_inc(c_stored, 16)
                sp_eng.wait_ge(dt_proj, b * ND + 1)
                load_wdt(2, 0)
                sp_eng.wait_ge(c_stored, b * 16 + 16)
                for p in range(NP):
                    sp_eng.dma_start(c_row[:, 4 * p:4 * p + 4, :],
                                     c_dram[4 * p:4 * p + 4, :].unsqueeze(0).broadcast_to([P, 4, T])
                                     ).then_inc(c_loaded[p], 16)

                def weights(d, par):
                    sp_eng.wait_ge(r_proj, b * ND + d + 1)
                    load_wres(d + 2, par)
                    sp_eng.wait_ge(dt_proj, b * ND + d + 2)
                    load_wdt(d + 3, 1 - par)

                with sp_eng.Fori(0, (ND - 4) // 2) as j:
                    for par in range(2):
                        weights(j * 2 + par, par)
                weights(ND - 4, 0)
                sp_eng.wait_ge(r_proj, b * ND + ND - 2)
                load_wres(ND - 1, 1)
                if not last:
                    for d in range(2):
                        sp_eng.wait_ge(dt_proj, b * ND + ND - 1 + d)
                        load_wdt(d, d)
                    for d in range(2):
                        sp_eng.wait_ge(r_proj, b * ND + ND - 1 + d)
                        load_wres(d, d)
                    sp_eng.dma_start(xt[:], x_t[b + 1]).then_inc(xt_loaded, 16)
                sp_eng.wait_ge(summed, b * (ND * NP) + ND * NP + NP)
                for tb in range(TT):
                    sp_eng.dma_start(ring[:, tb, 0, :], x[b, tb * P:(tb + 1) * P, :]).then_inc(x_loaded, 16)
                for tb in range(TT):
                    sp_eng.wait_ge(normed, b * TT + tb + 1)
                    sp_eng.dma_start(x1[b, tb * P:(tb + 1) * P, :], ring[:, tb, 0, :]).then_inc(stored, 16)

            sp_eng.nop().then_inc(stored, 16)
            with sp_eng.Fori(0, NB - 1) as b:
                row(b)
            row(NB - 1, last=True)
            sp_eng.wait_ge(stored, NB * TT * 16 + 16)

        @block.tensor
        def _(pe):
            pe.wait_ge(w_loaded, 16 * len(loads))

            def dt_product(b, d, par):
                pe.wait_ge(wdt_loaded[par], b * (8 * ND) + (d - par) * 8 + 16)
                nc.tensor.matmul(ps[:, DT_BANK, :], wdt_s[par][:], xdbl[:], start=True,
                                 stop=True).then_inc(dt_proj, 1)

            def res_product(b, d, par, bank, kts):
                pe.wait_ge(wres_loaded[par], b * (8 * ND) + (d - par) * 8 + 16)
                if bank == BT_BANK:
                    pe.wait_ge(vt_ready, b * ND + d + 1)
                for kt in kts:
                    m = nc.tensor.matmul(ps[:, bank, :], wres_s[par][:, kt, :], xt[:, kt, :], start=(kt == 0),
                                         stop=(kt == KT - 1))
                if kts[-1] == KT - 1:
                    m.then_inc(r_proj, 1)

            def v_transposes(b, d):
                if not (isinstance(d, int) and d == 0):
                    pe.wait_ge(r_taken, b * ND + d)
                pe.wait_ge(v_ready, b * ND + d + 1)
                for tb in range(TT):
                    m = nc.tensor.transpose(ps[:, BT_BANK, tb * P:(tb + 1) * P], v[:, tb * P:(tb + 1) * P],
                                            ident[:])
                m.then_inc(vt_proj, 1)

            def b_products(b, d, par, k):
                s = k % 2
                if k == 0:
                    pe.wait_ge(vt_ready, b * ND + d + 1)
                pe.wait_ge(scanned, b * (ND * NU) + d * NU + k + 1)
                for tb in range(TT):
                    for i in range(2):
                        m = nc.tensor.matmul(ps[:, 2 * s + i, tb * P:(tb + 1) * P],
                                             v_t[par][:, tb * P:(tb + 1) * P], diag_b[:, tb, 2 * k + i, :],
                                             start=True, stop=True)
                m.then_inc(dbu_ready, 1)

            def state_sum(b, d, par, p):
                if p == 0:
                    pe.wait_ge(y_taken, b * ND + d + 1)
                pe.wait_ge(folded, b * (ND * NP) + d * NP + p + 1)
                nc.tensor.matmul(ps[:, 4 + par, :], ident[:], ring[:, 2 * p, 0, :], start=(p == 0),
                                 stop=(p == NP - 1)).then_inc(summed, 1)

            def step(b, d, par, p, nxt=True, more=True):
                if p == LEAD and more:
                    pe.wait_ge(delta_ready, b * ND + d + 2)
                    dt_product(b, d + 2, par)
                ahead = (d, par, p + LEAD) if p + LEAD < NP else (d + 1, 1 - par, p + LEAD - NP)
                run = p + LEAD < NP or nxt
                if run:
                    b_products(b, ahead[0], ahead[1], 2 * ahead[2])
                if p > 0:
                    state_sum(b, d, par, p - 1)
                elif not (isinstance(d, int) and d == 0):
                    state_sum(b, d - 1, 1 - par, NP - 1)
                half = (p - LEAD) * 2
                if p >= LEAD and nxt:
                    res_product(b, d + 1, 1 - par, BT_BANK, [half])
                if run:
                    b_products(b, ahead[0], ahead[1], 2 * ahead[2] + 1)
                if p >= LEAD and nxt:
                    res_product(b, d + 1, 1 - par, BT_BANK, [half + 1])

            def out_product(b, tb, ds):
                for d in ds:
                    m = nc.tensor.matmul(ps[:, 6 + tb % 2, :], u[:, d, tb * P:(tb + 1) * P], wout[:, d, :],
                                         start=(d == 0), stop=(d == ND - 1))
                if ds[-1] == ND - 1:
                    m.then_inc(o_proj, 1)

            def channel_block(b, d, par, nxt=True, more=True):
                for p in range(LEAD, NP):
                    if not nxt:
                        pe.wait_ge(yg_ready, b * ND + ND - 2 + 1)
                        out_product(b, p - LEAD, range(ND - 2) if p == LEAD else range(ND // 2))
                    step(b, d, par, p, nxt, more)
                if nxt:
                    for p in range(LEAD):
                        step(b, d + 1, 1 - par, p)
                else:
                    state_sum(b, d, par, NP - 1)
                if more:
                    v_transposes(b, d + 2)

            nc.tensor.nop().then_inc(summed, NP)
            with pe.Fori(0, NB) as b:
                pe.wait_ge(xt_loaded, b * 16 + 16)
                for j in range(ND):
                    if j >= 4:
                        pe.wait_ge(taps, b * (ND * (TAPS - 1)) + (j - 3) * (TAPS - 1))
                    for kt in range(KT):
                        m = nc.tensor.matmul(ps[:, j % 4, :], wu[:, kt, j * P:(j + 1) * P], xt[:, kt, :],
                                             start=(kt == 0), stop=(kt == KT - 1))
                    m.then_inc(u_proj, 1)
                pe.wait_ge(w_rest_loaded, 16 * len(rest_loads))
                for j in range(ND):
                    pe.wait_ge(u_ready, b * ND + j + 1)
                    m = nc.tensor.matmul(ps[:, BT_BANK, :], wx[:, j, :], u[:, j, :], start=(j == 0),
                                         stop=(j == ND - 1))
                m.then_inc(x_proj, 1)
                pe.wait_ge(xdbl_ready, b + 1)
                dt_product(b, 0, 0)
                for tb in range(TT):
                    m = nc.tensor.matmul(ps[:, BT_BANK, tb * P:tb * P + NS], xdbl[:, tb * P:(tb + 1) * P],
                                         ident[:, B0:B0 + NS], start=True, stop=True)
                m.then_inc(bt_proj, 1)
                res_product(b, 0, 0, 5, range(KT))
                pe.wait_ge(bcol_ready, b + 1)
                v_transposes(b, 0)
                pe.wait_ge(delta_ready, b * ND + 1)
                dt_product(b, 1, 1)
                pe.wait_ge(diag_dve, b * 2 + 2)
                pe.wait_ge(diag_pool, b * 2 + 2)
                for k in range(2 * LEAD):
                    b_products(b, 0, 0, k)
                for p in range(LEAD):
                    step(b, 0, 0, p)
                v_transposes(b, 1)
                with pe.Fori(0, ND // 2 - 1) as j:
                    for par in range(2):
                        channel_block(b, j * 2 + par, par)
                channel_block(b, ND - 2, 0, more=False)
                channel_block(b, ND - 1, 1, nxt=False, more=False)
                out_product(b, 1, range(ND // 2, ND - 2))
                pe.wait_ge(yg_ready, b * ND + ND)
                for tb in range(2):
                    out_product(b, tb, [ND - 2])
                pe.wait_ge(yg_ready, b * ND + ND + 1)
                for tb in range(TT):
                    if tb < 2:
                        out_product(b, tb, [ND - 1])
                    else:
                        pe.wait_ge(z_done, b * TT + tb - 1)
                        out_product(b, tb, range(ND))

        @block.scalar
        def _(act):
            act.wait_ge(w_loaded, 16 * len(loads))
            nc.scalar.activation(a_neg[:], a_neg[:], ACT.Exp).then_inc(a_exp, 1)
            act.wait_ge(consts, 3)

            def softplus(b, d):
                act.wait_ge(dt_proj, b * ND + d + 1)
                if not (isinstance(d, int) and d == 0):
                    act.wait_ge(delta_ready, b * ND + d)
                nc.scalar.activation(sp_e[:], ps[:, DT_BANK, :], ACT.Abs).then_inc(sp, 1)
                act.wait_ge(sp, b * (4 * ND) + d * 4 + 1)
                nc.scalar.activation(sp_e[:], sp_e[:], ACT.Exp, scale=-1.0).then_inc(sp, 1)
                act.wait_ge(sp, b * (4 * ND) + d * 4 + 2)
                nc.scalar.activation(sp_s[:], sp_e[:], ACT.Square, scale=0.5 ** 0.5)
                nc.scalar.activation(sp_w[:], sp_e[:], ACT.Identity, bias=1.0).then_inc(sp, 1)
                nc.scalar.activation(sp_l[:], sp_e[:], ACT.Ln, bias=1.0).then_inc(sp, 1)

            def take_vt(b, d, par):
                act.wait_ge(vt_proj, b * ND + d + 1)
                nc.scalar.copy(v_t[par][:], ps[:, BT_BANK, :]).then_inc(vt_ready, 1)

            def decay(b, d, par, k):
                if k == 0:
                    act.wait_ge(delta_ready, b * ND + d + 1)
                if k % 2 == 0:
                    act.wait_ge(summed, b * (ND * NP) + d * NP + k // 2 + 1)
                nc.scalar.copy(ring[:, k, :, 0:1], zero2[:])
                for i in range(2):
                    a = nc.scalar.activation(ring[:, k, i, 1:], delta[par][:, 1:], ACT.Exp,
                                             scale=a_neg[:, d, 2 * k + i:2 * k + i + 1])
                a.then_inc(da_ready, 1)

            def take_res(b, d, par, bank):
                act.wait_ge(r_proj, b * ND + d + 1)
                if bank == BT_BANK:
                    act.wait_ge(yg_ready, b * ND + d)
                nc.scalar.activation(gate[par][:], ps[:, bank, :], ACT.Silu).then_inc(r_taken, 1)

            def step(b, d, par, p, nxt=True, more=True):
                if p == NP - 1 and more:
                    softplus(b, d + 2)
                if p + LEAD < NP:
                    decay(b, d, par, 2 * (p + LEAD))
                    decay(b, d, par, 2 * (p + LEAD) + 1)
                elif nxt:
                    decay(b, d + 1, 1 - par, 2 * (p + LEAD - NP))
                    decay(b, d + 1, 1 - par, 2 * (p + LEAD - NP) + 1)
                if p == NP - 1 and nxt:
                    take_res(b, d + 1, 1 - par, BT_BANK)

            def channel_block(b, d, par, nxt=True, more=True):
                for p in range(LEAD, NP):
                    step(b, d, par, p, nxt, more)
                if nxt:
                    for p in range(LEAD):
                        step(b, d + 1, 1 - par, p)
                if more:
                    take_vt(b, d + 2, par)

            with act.Fori(0, NB) as b:
                def silu_u(j):
                    act.wait_ge(taps, b * (ND * (TAPS - 1)) + (j + 1) * (TAPS - 1))
                    nc.scalar.activation(u[:, j, :], u[:, j, :], ACT.Silu).then_inc(u_ready, 1)

                for j in range(ND):
                    act.wait_ge(u_proj, b * ND + j + 1)
                    nc.scalar.activation(u[:, j, :], ps[:, j % 4, :], ACT.Identity, bias=bcv[:, j:j + 1],
                                         scale=wcv[:, j, TAPS - 1:TAPS]).then_inc(tap_last, 1)
                    if j >= 1:
                        silu_u(j - 1)
                silu_u(ND - 1)
                act.wait_ge(x_proj, b + 1)
                nc.scalar.activation(xdbl[:], ps[:, BT_BANK, :], ACT.Identity,
                                     bias=ident[:, DTR:DTR + 1]).then_inc(xdbl_ready, 1)
                softplus(b, 0)
                take_res(b, 0, 0, 5)
                take_vt(b, 0, 0)
                act.wait_ge(stored, b * (16 * TT) + 16)
                for k in range(2 * LEAD):
                    decay(b, 0, 0, k)
                softplus(b, 1)
                for p in range(LEAD):
                    step(b, 0, 0, p)
                take_vt(b, 1, 1)
                with act.Fori(0, ND // 2 - 1) as j:
                    for par in range(2):
                        channel_block(b, j * 2 + par, par)
                channel_block(b, ND - 2, 0, more=False)
                channel_block(b, ND - 1, 1, nxt=False, more=False)
                act.wait_ge(stats, b * (2 * TT) + 2 * TT)
                nc.scalar.activation(rstd[:], mv[:, :, 1], ACT.Ln, bias=eps[:]).then_inc(rstd_ln, 1)
                act.wait_ge(rstd_ln, b + 1)
                nc.scalar.activation(rstd[:], rstd[:], ACT.Exp, scale=-0.5).then_inc(rstd_ready, 1)

        @block.vector
        def _(dve):
            dve.wait_ge(a_exp, 1)
            nc.vector.tensor_scalar(a_neg[:], a_neg[:], -1.0, None, ALU.mult).then_inc(consts, 1)
            nc.vector.memset(eps[:], EPS).then_inc(consts, 1)
            nc.vector.memset(zero2[:], 0.0).then_inc(consts, 1)
            dve.wait_ge(consts, 3)
            nc.vector.nop().then_inc(scanned, 2)
            nc.vector.nop().then_inc(y_taken, 2)

            def scan(b, d, par, k):
                dve.wait_ge(dbu_ready, b * (ND * NU) + d * NU + k + 1)
                dve.wait_ge(da_ready, b * (ND * NU) + d * NU + k + 1)
                s = k % 2
                slot = ring[:, k].rearrange("p a t -> p (a t)")
                nc.vector.tensor_tensor_scan(slot, slot, ps[:, 2 * s:2 * s + 2, :].rearrange("p a t -> p (a t)"),
                                             0.0, ALU.mult, ALU.add).then_inc(scanned, 1)

            def times_c(b, d, p):
                k = 2 * p + 1
                if p >= LEAD or isinstance(d, int) and d == 0:
                    dve.wait_ge(c_loaded[p], b * 16 + 16)
                dve.wait_ge(scanned, b * (ND * NU) + d * NU + k + 3)
                nc.vector.tensor_tensor(ring[:, k], ring[:, k], c_row[:, 2 * k:2 * k + 2, :],
                                        ALU.mult).then_inc(c_dve, 1)

            def fold(b, d, p):
                dve.wait_ge(paired, b * (ND * NP) + d * NP + p + 1)
                nc.vector.tensor_tensor(ring[:, 2 * p, 0, :], ring[:, 2 * p, 0, :], ring[:, 2 * p, 1, :],
                                        ALU.add).then_inc(folded, 1)

            def softplus(b, d, par, i):
                n = b * (4 * ND) + d * 4
                if i == 0:
                    dve.wait_ge(sp, b * (4 * ND) + d * 4 + 3)
                    nc.vector.scalar_tensor_tensor(v[:], sp_w[:], -1.0, sp_e[:], ALU.add, ALU.subtract).then_inc(sq, 1)
                elif i == 1:
                    nc.vector.scalar_tensor_tensor(sp_s[:], sp_s[:], -1.0, sp_e[:], ALU.mult,
                                                   ALU.add).then_inc(sq, 1)
                elif i == 2:
                    dve.wait_ge(sp, b * (4 * ND) + d * 4 + 4)
                    dve.wait_ge(sq, n + 1)
                    nc.vector.scalar_tensor_tensor(v[:], sp_l[:], -LN_SLACK, v[:], ALU.add,
                                                   ALU.subtract).then_inc(sq, 1)
                elif i == 3:
                    dve.wait_ge(sq, n + 3)
                    nc.vector.tensor_tensor(sp_s[:], sp_s[:], v[:], ALU.max).then_inc(sq, 1)
                else:
                    dve.wait_ge(sq, n + 4)
                    nc.vector.scalar_tensor_tensor(delta[par][:], ps[:, DT_BANK, :], 0.0, sp_s[:], ALU.max,
                                                   ALU.add).then_inc(delta_ready, 1)

            def take_y(b, d, par):
                dve.wait_ge(summed, b * (ND * NP) + d * NP + NP + NP)
                nc.vector.scalar_tensor_tensor(u[:, d, :], u[:, d, :], dsk[:, bass.ds(d, 1)], ps[:, 4 + par, :],
                                               ALU.mult, ALU.add).then_inc(y_taken, 1)

            def step(b, d, par, p, nxt=True, more=True):
                ahead = (d, par, p + LEAD) if p + LEAD < NP else (d + 1, 1 - par, p + LEAD - NP)
                run = p + LEAD < NP or nxt
                if run:
                    scan(b, *ahead[:2], 2 * ahead[2])
                fold(b, d, p)
                if p == NP - 1 and more:
                    for i in range(2):
                        softplus(b, d + 2, par, i)
                if run:
                    scan(b, *ahead[:2], 2 * ahead[2] + 1)
                if p == NP - 1 and more:
                    for i in range(2, 4):
                        softplus(b, d + 2, par, i)
                if run:
                    times_c(b, ahead[0], ahead[2])

            def channel_block(b, d, par, nxt=True, more=True):
                for p in range(LEAD, NP):
                    step(b, d, par, p, nxt, more)
                if nxt:
                    for p in range(LEAD):
                        if p == 0 and more:
                            softplus(b, d + 2, par, 4)
                        step(b, d + 1, 1 - par, p)
                take_y(b, d, par)

            with dve.Fori(0, NB) as b:
                for j in range(ND):
                    for c in range(TAPS - 1):
                        lag = c + 1
                        if c == 0:
                            dve.wait_ge(tap_last, b * ND + j + 1)
                        else:
                            dve.wait_ge(taps, b * (ND * (TAPS - 1)) + j * (TAPS - 1) + c)
                        nc.vector.scalar_tensor_tensor(u[:, j, lag:], ps[:, j % 4, 0:T - lag],
                                                       wcv[:, j, TAPS - 1 - lag:TAPS - lag], u[:, j, lag:],
                                                       ALU.mult, ALU.add).then_inc(taps, 1)
                dve.wait_ge(w_rest_loaded, 16 * len(rest_loads))
                dve.wait_ge(bt_proj, b + 1)
                nc.vector.tensor_copy(b_col[:], ps[:, BT_BANK, :].rearrange("p (a c) -> p a c", a=TT)[:, :, 0:NS]
                                      ).then_inc(bcol_ready, 1)
                dve.wait_ge(bcol_ready, b + 1)
                for tb in (0, 1):
                    nc.vector.tensor_tensor(diag_b[:, tb], ident[:].unsqueeze(1).broadcast_to([P, NS, P]),
                                            b_col[:, tb, :].unsqueeze(2).broadcast_to([P, NS, P]),
                                            ALU.mult).then_inc(diag_dve, 1)
                    if tb == 0:
                        for i in range(5):
                            softplus(b, 0, 0, i)
                        dve.wait_ge(delta_ready, b * ND + 1)
                        nc.vector.tensor_tensor(v[:], delta[0][:], u[:, 0, :], ALU.mult).then_inc(v_ready, 1)
                for p in range(LEAD):
                    scan(b, 0, 0, 2 * p)
                    scan(b, 0, 0, 2 * p + 1)
                    times_c(b, 0, p)
                for i in range(5):
                    softplus(b, 1, 1, i)
                for p in range(LEAD):
                    step(b, 0, 0, p)
                with dve.Fori(0, ND // 2 - 1) as j:
                    for par in range(2):
                        channel_block(b, j * 2 + par, par)
                channel_block(b, ND - 2, 0, more=False)
                channel_block(b, ND - 1, 1, nxt=False, more=False)
                dve.wait_ge(x_loaded, b * (16 * TT) + 16 * TT)
                for tb in range(TT):
                    dve.wait_ge(o_proj, b * TT + tb + 1)
                    nc.vector.tensor_tensor(ring[:, tb, 0, :], ps[:, 6 + tb % 2, :], ring[:, tb, 0, :],
                                            ALU.add).then_inc(z_done, 1)
                    dve.wait_ge(z_done, b * TT + tb + 1)
                    nc.vector.bn_stats(st6[:, tb, :], ring[:, tb, 0, :]).then_inc(stats, 1)
                    dve.wait_ge(stats, b * (2 * TT) + 2 * tb + 1)
                    nc.vector.tensor_copy(tick[:], eps[:])
                    nc.vector.bn_aggr(mv[:, tb, :], st6[:, tb, :]).then_inc(stats, 1)
                dve.wait_ge(rstd_ready, b + 1)
                for tb in range(TT):
                    nc.vector.tensor_scalar(ring[:, tb, 0, :], ring[:, tb, 0, :], mv[:, tb, 0:1], rstd[:, tb:tb + 1],
                                            ALU.subtract, ALU.mult).then_inc(normed, 1)

        @block.gpsimd
        def _(pool):
            pool.wait_ge(w_loaded, 16 * len(loads))

            def make_v(b, d, par):
                pool.wait_ge(delta_ready, b * ND + d + 1)
                nc.gpsimd.tensor_tensor(v[:], delta[par][:], u[:, d, :], ALU.mult).then_inc(v_ready, 1)

            def times_c(b, d, p):
                k = 2 * p
                if p >= LEAD or isinstance(d, int) and d == 0:
                    pool.wait_ge(c_loaded[p], b * 16 + 16)
                pool.wait_ge(scanned, b * (ND * NU) + d * NU + k + 3)
                nc.gpsimd.tensor_tensor(ring[:, k], ring[:, k], c_row[:, 2 * k:2 * k + 2, :],
                                        ALU.mult).then_inc(c_pool, 1)

            def add_pair(b, d, p):
                k = 2 * p
                pool.wait_ge(c_pool, b * (ND * NP) + d * NP + p + 1)
                pool.wait_ge(c_dve, b * (ND * NP) + d * NP + p + 1)
                nc.gpsimd.tensor_tensor(ring[:, k], ring[:, k], ring[:, k + 1], ALU.add).then_inc(paired, 1)

            def gate_y(b, d, par):
                pool.wait_ge(y_taken, b * ND + d + 3)
                pool.wait_ge(r_taken, b * ND + d + 1)
                nc.gpsimd.tensor_tensor(u[:, d, :], gate[par][:], u[:, d, :], ALU.mult).then_inc(yg_ready, 1)

            def step(b, d, par, p, nxt=True, more=True):
                if p + 1 < NP:
                    add_pair(b, d, p + 1)
                elif nxt:
                    add_pair(b, d + 1, 0)
                if p + LEAD < NP:
                    times_c(b, d, p + LEAD)
                elif nxt:
                    times_c(b, d + 1, p + LEAD - NP)

            def channel_block(b, d, par, nxt=True, more=True):
                for p in range(LEAD, NP):
                    step(b, d, par, p, nxt, more)
                if nxt:
                    for p in range(LEAD):
                        if p == 0 and more:
                            make_v(b, d + 2, par)
                        step(b, d + 1, 1 - par, p)
                gate_y(b, d, par)

            nc.gpsimd.nop().then_inc(yg_ready, 1)
            with pool.Fori(0, NB) as b:
                pool.wait_ge(bcol_ready, b + 1)
                for tb in (2, 3):
                    nc.gpsimd.tensor_tensor(diag_b[:, tb], ident[:].unsqueeze(1).broadcast_to([P, NS, P]),
                                            b_col[:, tb, :].unsqueeze(2).broadcast_to([P, NS, P]),
                                            ALU.mult).then_inc(diag_pool, 1)
                times_c(b, 0, 0)
                add_pair(b, 0, 0)
                times_c(b, 0, 1)
                make_v(b, 1, 1)
                for p in range(LEAD):
                    step(b, 0, 0, p)
                with pool.Fori(0, ND // 2 - 1) as j:
                    for par in range(2):
                        channel_block(b, j * 2 + par, par)
                channel_block(b, ND - 2, 0, more=False)
                channel_block(b, ND - 1, 1, nxt=False, more=False)


def cross_attention_ffn_pass(nc, x1, ctx_t, attn_mask, pad_mask, wq, wk, wv, wo, bq, bk, bv, bo,
                             wr, wkf, wvf, mu_r, mu_k, ident_d, out):
    NB, T, DM = x1.shape
    NK = ctx_t.shape[2] // NB
    KT = DM // P
    TT = T // P
    DK = 32
    NH = DM // DK
    HB = P // DK
    HW = HB * NK
    SCALE = 1.0 / DK ** 0.5
    MASKED = -3e38
    LIVE = -1e38
    KB = 4
    SETUP_A, SETUP_V = KT * (NB // KB), NB
    FRONT, FFN, ATTEND = 2 * KT, 3 * KT, NH + KT
    ROW_A = FRONT + FFN + ATTEND
    ROW_V = TT * KT + TT + TT

    def front_a(b):
        return SETUP_A if isinstance(b, int) and b == 0 else b * ROW_A + (SETUP_A - FFN)

    def attend_a(b):
        return b * ROW_A + (SETUP_A + FRONT)

    def scores_v(b):
        return SETUP_V if isinstance(b, int) and b == 0 else b * ROW_V + (SETUP_V - TT)

    def out_v(b):
        return b * ROW_V + (SETUP_V + TT * KT)

    LAST_A, LAST_V = attend_a(NB - 1) + ATTEND, out_v(NB - 1) + TT

    ctx = ExitStack()
    with ctx:
        def sb(name, shape, dt=FP32):
            return ctx.enter_context(nc.sbuf_tensor("xf_" + name, shape, dt))

        def sem(name):
            return ctx.enter_context(nc.semaphore("xf_" + name))

        def wait_at_least(eng, s, value):
            if not (isinstance(value, int) and value <= 0):
                eng.wait_ge(s, value)

        wq_s, wo_s, wr_s, wkf_s, wvf_s = (sb(n, [P, KT, DM]) for n in ("wq", "wo", "wr", "wkf", "wvf"))
        kbd = sb("kbd", [P, NB, KT, HW])
        v_all = sb("v_all", [P, NB, DM])
        v_cur = sb("v_cur", [P, DM])
        xn = [sb(f"xn{i}", [P, TT, DM]) for i in range(2)]
        x1t = sb("x1t", [P, KT, T])
        kf = ot = x1t
        qt = sb("qt", [P, KT, T])
        pr = sb("pr", [P, TT, NH, NK])
        pt = sb("pt", [P, 2 * HB, T])
        x2t = sb("x2t", [P, KT, T + 1])
        xr, xk = sb("xr", [P, KT, T]), sb("xk", [P, KT, T])
        r_s = sb("r_s", [P, TT, DM])
        ctx_s = pt[:].rearrange("p a t -> p (a t)")[:, 0:KT * NB * NK].rearrange("p (k n) -> p k n", k=KT)
        wk_s, wv_s, bv_s = xr, xk, r_s[:, 0, :]
        bo_s = sb("bo_s", [P, DM])
        bq_s, bk_s, mur, muk, omr, omk = (sb(n, [P, KT]) for n in ("bq", "bk", "mur", "muk", "omr", "omk"))
        am_u, pm_u = sb("am_u", [P, TT, NK], U8), sb("pm_u", [P, NB, NK], U8)
        am, pm = sb("am", [P, TT, NK]), sb("pm", [P, NB, NK])
        mask = sb("mask", [P, TT, NK])
        ident = sb("ident", [P, P])
        eps = sb("eps", [P, 1])
        tick = sb("tick", [P, 1])
        top, total, live = (sb(n, [P, TT, NH]) for n in ("top", "total", "live"))
        st6, mv, rstd = sb("st6", [P, TT, 6]), sb("mv", [P, TT, 2]), sb("rstd", [P, TT])
        gst6, gmv, grstd = sb("gst6", [P, TT, 6]), sb("gmv", [P, TT, 2]), sb("grstd", [P, TT])

        ps = ctx.enter_context(nc.psum_tensor("xf_ps", [P, 8, T], FP32))

        kv_loaded = sem("kv_loaded")
        w_loaded = sem("w_loaded")
        x_loaded = [sem(f"x_loaded{i}") for i in range(2)]
        zeroed = sem("zeroed")
        consts = sem("consts")
        a_filled, a_taken = sem("a_filled"), sem("a_taken")
        v_filled, v_taken = sem("v_filled"), sem("v_taken")
        biased = sem("biased")
        v_here = sem("v_here")
        masked = sem("masked")
        topped = sem("topped")
        centred = sem("centred")
        exped = sem("exped")
        shares = sem("shares")
        probs = sem("probs")
        scaled = sem("scaled")
        mixed = sem("mixed")
        squared = sem("squared")
        z2_stats = sem("z2_stats")
        rstd2_ln, rstd2 = sem("rstd2_ln"), sem("rstd2")
        normed2 = sem("normed2")
        z3 = sem("z3")
        z3_stats = sem("z3_stats")
        rstd3_ln, rstd3 = sem("rstd3_ln"), sem("rstd3")
        normed3 = sem("normed3")
        stored = sem("stored")

        block = ctx.enter_context(nc.Block())

        def rows(body, eng):
            body(0, 0)
            with eng.Fori(0, (NB - 2) // 2) as i:
                for s in range(2):
                    body(i * 2 + (1 + s), 1 - s)
            body(NB - 1, (NB - 1) % 2)

        kv_loads = [(wk_s[:], wk), (ctx_s, ctx_t), (bk_s[:], bk), (wv_s[:], wv),
                 (bv_s, bv.unsqueeze(0).broadcast_to([P, DM])), (ident[:], ident_d)]
        loads = [(wq_s[:], wq), (bq_s[:], bq),
                 (am_u[:], attn_mask), (pm_u[:], pad_mask.unsqueeze(0).broadcast_to([P, NB, NK])),
                 (bo_s[:], bo.unsqueeze(0).broadcast_to([P, DM])), (wo_s[:], wo), (mur[:], mu_r), (muk[:], mu_k),
                 (wr_s[:], wr), (wkf_s[:], wkf), (wvf_s[:], wvf)]

        @block.sync
        def _(sp):
            def load(b, par):
                for tb in range(TT):
                    sp.dma_start(xn[par][:, tb, :], x1[b, tb * P:(tb + 1) * P, :]).then_inc(x_loaded[par], 16)

            def store(b, par):
                for tb in range(TT):
                    sp.wait_ge(normed3, b * TT + tb + 1)
                    sp.dma_start(out[b, tb * P:(tb + 1) * P, :], xn[par][:, tb, :]).then_inc(stored, 16)

            for dst, src in kv_loads:
                sp.dma_start(dst, src).then_inc(kv_loaded, 16)
            load(0, 0)
            for dst, src in loads:
                sp.dma_start(dst, src).then_inc(w_loaded, 16)

            def row(b, par):
                if isinstance(b, int) and b == 0:
                    load(1, 1)
                    return
                store(b - 1, 1 - par)
                if not (isinstance(b, int) and b == NB - 1):
                    sp.wait_ge(stored, b * (16 * TT))
                    load(b + 1, 1 - par)

            rows(row, sp)
            store(NB - 1, (NB - 1) % 2)
            sp.wait_ge(stored, NB * TT * 16)

        @block.tensor
        def _(pe):
            pe.wait_ge(kv_loaded, 16 * len(kv_loads))

            def a_bank(a):
                wait_at_least(pe, a_taken, a - 4)

            def v_bank(v):
                wait_at_least(pe, v_taken, v - 4)

            def product_a(a, i, lhs_t, rhs):
                a_bank(a + (i + 1))
                for kt in range(KT):
                    m = nc.tensor.matmul(ps[:, i % 4, :], lhs_t(kt), rhs(kt), start=(kt == 0), stop=(kt == KT - 1))
                m.then_inc(a_filled, 1)

            def product_v(v, i, lhs_t, rhs):
                v_bank(v + (i + 1))
                for kt in range(KT):
                    m = nc.tensor.matmul(ps[:, 4 + i % 4, :], lhs_t(kt), rhs(kt), start=(kt == 0), stop=(kt == KT - 1))
                m.then_inc(v_filled, 1)

            def transposed(a, i, source):
                a_bank(a + (i + 1))
                for tb in range(TT):
                    m = nc.tensor.transpose(ps[:, i % 4, tb * P:(tb + 1) * P], source[:, tb, i * P:(i + 1) * P],
                                            ident[:])
                m.then_inc(a_filled, 1)

            def front(b, par):
                a = front_a(b)
                pe.wait_ge(x_loaded[par], (b - par) * (8 * TT) + 16 * TT)
                for kt in range(KT):
                    transposed(a, kt, xn[par])
                pe.wait_ge(a_taken, a + KT)
                for j in range(KT):
                    product_a(a, KT + j, lambda kt: wq_s[:, kt, j * P:(j + 1) * P], lambda kt: x1t[:, kt, :])

            def x2_transposes(b, a, par):
                pe.wait_ge(normed2, b * TT + TT)
                for kt in range(KT):
                    transposed(a, kt, xn[par])

            def scores(b, tb):
                v = scores_v(b)
                if tb == 0:
                    pe.wait_ge(a_taken, front_a(b) + 2 * KT)
                for j in range(KT):
                    v_bank(v + (tb * KT + j + 1))
                    nc.tensor.matmul(ps[:, 4 + j, 0:HW], qt[:, j, tb * P:(tb + 1) * P], kbd[:, b, j, :],
                                     start=True, stop=True).then_inc(v_filled, 1)

            def ffn_k(a, j):
                product_a(a, KT + j, lambda kt: wkf_s[:, kt, j * P:(j + 1) * P], lambda kt: xk[:, kt, :])

            def ffn_r(a, tb):
                product_a(a, 2 * KT + tb, lambda kt: xr[:, kt, tb * P:(tb + 1) * P], lambda kt: wr_s[:, kt, :])

            def ffn_v(b, v):
                pe.wait_ge(squared, b * KT + KT)
                for tb in range(TT):
                    product_v(v, tb, lambda kt: kf[:, kt, tb * P:(tb + 1) * P], lambda kt: wvf_s[:, kt, :])

            def attend(b):
                a, v = attend_a(b), out_v(b)
                n = 0

                def values(j, n):
                    pe.wait_ge(a_taken, a + ends[j])
                    a_bank(a + (n + 1))
                    for i in range(HB):
                        h = j * HB + i
                        m = nc.tensor.matmul(ps[i * DK:(i + 1) * DK, n % 4, :], v_cur[0:NK, h * DK:(h + 1) * DK],
                                             pt[0:NK, h % (2 * HB), :], start=True, stop=True,
                                             tile_position=(0, i * DK))
                    m.then_inc(a_filled, 1)

                pe.wait_ge(probs, b * TT + TT)
                pe.wait_ge(v_here, b + 1)
                ends = []
                for j in range(KT):
                    for i in range(HB):
                        h = j * HB + i
                        a_bank(a + (n + 1))
                        for tb in range(TT):
                            m = nc.tensor.transpose(ps[0:NK, n % 4, tb * P:(tb + 1) * P], pr[:, tb, h, :], ident[:])
                        m.then_inc(a_filled, 1)
                        n += 1
                    ends.append(n)
                    if j >= 1:
                        values(j - 1, n)
                        n += 1
                values(KT - 1, n)
                for kts, ready in ((range(KT - 1), ATTEND - 1), (range(KT - 1, KT), ATTEND)):
                    pe.wait_ge(a_taken, a + ready)
                    for tb in range(TT):
                        if kts[0] == 0:
                            v_bank(v + (tb + 1))
                        for kt in kts:
                            m = nc.tensor.matmul(ps[:, 4 + tb, :], ot[:, kt, tb * P:(tb + 1) * P], wo_s[:, kt, :],
                                                 start=(kt == 0), stop=(kt == KT - 1))
                        if kts[-1] == KT - 1:
                            m.then_inc(v_filled, 1)

            for half in range(NB // KB):
                for j in range(KT):
                    i = half * KT + j
                    a_bank(i + 1)
                    for kt in range(KT):
                        m = nc.tensor.matmul(ps[:, j, 0:KB * NK], wk_s[:, kt, j * P:(j + 1) * P],
                                             ctx_s[:, kt, half * KB * NK:(half + 1) * KB * NK],
                                             start=(kt == 0), stop=(kt == KT - 1))
                    m.then_inc(a_filled, 1)
            for i in range(NB):
                v_bank(i + 1)
                for kt in range(KT):
                    m = nc.tensor.matmul(ps[0:NK, 4 + i % 4, :], ctx_s[:, kt, i * NK:(i + 1) * NK], wv_s[:, kt, :],
                                         start=(kt == 0), stop=(kt == KT - 1))
                m.then_inc(v_filled, 1)

            pe.wait_ge(w_loaded, 16 * len(loads))

            def row(b, par):
                first = isinstance(b, int) and b == 0
                front(b, par)
                scores(b, 0)
                if not first:
                    a = front_a(b) + FRONT
                    x2_transposes(b - 1, a, 1 - par)
                scores(b, 1)
                if not first:
                    pe.wait_ge(mixed, (b - 1) * (2 * KT) + KT)
                    ffn_k(a, 0)
                    ffn_k(a, 1)
                scores(b, 2)
                if not first:
                    ffn_k(a, 2)
                    ffn_k(a, 3)
                scores(b, 3)
                if not first:
                    pe.wait_ge(mixed, (b - 1) * (2 * KT) + 2 * KT)
                    for tb in range(TT):
                        ffn_r(a, tb)
                    ffn_v(b - 1, scores_v(b) + TT * KT)
                attend(b)

            rows(row, pe)
            x2_transposes(NB - 1, LAST_A, (NB - 1) % 2)
            pe.wait_ge(mixed, NB * (2 * KT))
            for j in range(KT):
                ffn_k(LAST_A, j)
            for tb in range(TT):
                ffn_r(LAST_A, tb)
            ffn_v(NB - 1, LAST_V)

        @block.scalar
        def _(act):
            act.wait_ge(kv_loaded, 16 * len(kv_loads))
            act.wait_ge(zeroed, 2)
            for half in range(NB // KB):
                for j in range(KT):
                    act.wait_ge(a_filled, half * KT + j + 1)
                    for i in range(HB):
                        r0 = i * DK
                        s = nc.scalar.activation(
                            kbd[r0:r0 + DK, half * KB:(half + 1) * KB, j, i * NK:(i + 1) * NK],
                            ps[r0:r0 + DK, j, 0:KB * NK].rearrange("p (b n) -> p b n", b=KB),
                            ACT.Identity, bias=bk_s[r0:r0 + DK, j:j + 1])
                    s.then_inc(a_taken, 1)
            act.wait_ge(w_loaded, 16 * len(loads))
            act.wait_ge(consts, 5)

            def front_x(b):
                a = front_a(b)
                for kt in range(KT):
                    act.wait_ge(a_filled, a + (kt + 1))
                    nc.scalar.copy(x1t[:, kt, :], ps[:, kt, :]).then_inc(a_taken, 1)

            def front_q(b):
                a = front_a(b)
                for j in range(KT):
                    act.wait_ge(a_filled, a + (KT + j + 1))
                    nc.scalar.activation(qt[:, j, :], ps[:, j, :], ACT.Identity,
                                         bias=bq_s[:, j:j + 1]).then_inc(a_taken, 1)

            def rstd_of(stats, n, var, dst, ln_done, done, b):
                act.wait_ge(stats, b * n + n)
                nc.scalar.activation(dst[:], var[:, :, 1], ACT.Ln, bias=eps[:]).then_inc(ln_done, 1)
                act.wait_ge(ln_done, b + 1)
                nc.scalar.activation(dst[:], dst[:], ACT.Exp, scale=-0.5).then_inc(done, 1)

            def take_x2(a):
                for kt in range(KT):
                    act.wait_ge(a_filled, a + (kt + 1))
                    nc.scalar.copy(x2t[:, kt, 1:], ps[:, kt, :]).then_inc(a_taken, 1)

            def scale_x2(a, dst, mu):
                for kt in range(KT):
                    act.wait_ge(a_taken, a + (kt + 1))
                    nc.scalar.activation(dst[:, kt, :], x2t[:, kt, 1:], ACT.Copy,
                                         scale=mu[:, kt:kt + 1]).then_inc(scaled, 1)

            def exp(b, tb):
                act.wait_ge(centred, b * TT + tb + 1)
                nc.scalar.activation(pr[:, tb], pr[:, tb], ACT.Exp).then_inc(exped, 1)

            def take_k(a, j):
                act.wait_ge(a_filled, a + (KT + j + 1))
                nc.scalar.activation(kf[:, j, :], ps[:, j, :], ACT.Relu).then_inc(a_taken, 1)

            def take_r(a, tb):
                act.wait_ge(a_filled, a + (2 * KT + tb + 1))
                nc.scalar.activation(r_s[:, tb, :], ps[:, tb, :], ACT.Sigmoid).then_inc(a_taken, 1)

            def rstd_ffn(b):
                rstd_of(z3_stats, 2 * TT, gmv, grstd, rstd3_ln, rstd3, b)

            def attend(b, before):
                a = attend_a(b)
                n = 0

                def values(j, n):
                    act.wait_ge(a_filled, a + (n + 1))
                    nc.scalar.copy(ot[:, j, :], ps[:, n % 4, :]).then_inc(a_taken, 1)

                for j in range(KT):
                    for i in range(HB):
                        h = j * HB + i
                        act.wait_ge(a_filled, a + (n + 1))
                        nc.scalar.copy(pt[0:NK, h % (2 * HB), :], ps[0:NK, n % 4, :]).then_inc(a_taken, 1)
                        n += 1
                    if j >= 1:
                        values(j - 1, n)
                        n += 1
                values(KT - 1, n)
                if before:
                    rstd_ffn(b - 1)

            def row(b, par):
                first = isinstance(b, int) and b == 0
                front_x(b)
                if not first:
                    rstd_of(z2_stats, 2 * TT, mv, rstd, rstd2_ln, rstd2, b - 1)
                front_q(b)
                a = front_a(b) + FRONT
                if not first:
                    take_x2(a)
                    scale_x2(a, xk, muk)
                exp(b, 0)
                if not first:
                    scale_x2(a, xr, mur)
                    take_k(a, 0)
                    take_k(a, 1)
                exp(b, 1)
                if not first:
                    take_k(a, 2)
                    take_k(a, 3)
                exp(b, 2)
                exp(b, 3)
                if not first:
                    for tb in range(TT):
                        take_r(a, tb)
                attend(b, not first)

            rows(row, act)
            rstd_of(z2_stats, 2 * TT, mv, rstd, rstd2_ln, rstd2, NB - 1)
            take_x2(LAST_A)
            scale_x2(LAST_A, xk, muk)
            scale_x2(LAST_A, xr, mur)
            for j in range(KT):
                take_k(LAST_A, j)
            for tb in range(TT):
                take_r(LAST_A, tb)
            rstd_ffn(NB - 1)

        @block.vector
        def _(dve):
            dve.wait_ge(kv_loaded, 16 * len(kv_loads))
            for i in range(NB):
                dve.wait_ge(v_filled, i + 1)
                nc.vector.tensor_tensor(v_all[0:NK, i, :], ps[0:NK, 4 + i % 4, :], bv_s[0:NK, :],
                                        ALU.add).then_inc(v_taken, 1)
            dve.wait_ge(w_loaded, 16 * len(loads))
            nc.vector.tensor_scalar(am[:], am_u[:], MASKED, None, ALU.mult).then_inc(consts, 1)
            nc.vector.tensor_scalar(pm[:], pm_u[:], MASKED, None, ALU.mult).then_inc(consts, 1)
            nc.vector.tensor_scalar(omr[:], mur[:], -1.0, 1.0, ALU.mult, ALU.add).then_inc(consts, 1)
            nc.vector.tensor_scalar(omk[:], muk[:], -1.0, 1.0, ALU.mult, ALU.add).then_inc(consts, 1)
            nc.vector.memset(eps[:], EPS).then_inc(consts, 1)
            dve.wait_ge(consts, 5)
            dve.wait_ge(zeroed, 2)

            def mix(b, which):
                dst, om = ((xk, omk), (xr, omr))[which]
                for kt in range(KT):
                    dve.wait_ge(scaled, b * (2 * KT) + (which * KT + kt + 1))
                    nc.vector.scalar_tensor_tensor(dst[:, kt, :], x2t[:, kt, 0:T], om[:, kt:kt + 1], dst[:, kt, :],
                                                   ALU.mult, ALU.add).then_inc(mixed, 1)

            def shares_of(b, tb):
                n = (b * TT + tb) * 4
                dve.wait_ge(exped, b * TT + tb + 1)
                nc.vector.tensor_reduce(total[:, tb], pr[:, tb], AX.X, ALU.add).then_inc(shares, 1)
                nc.vector.tensor_scalar(live[:, tb], top[:, tb], LIVE, None, ALU.is_gt).then_inc(shares, 1)
                dve.wait_ge(shares, n + 2)
                nc.vector.tensor_tensor(total[:, tb], total[:, tb], live[:, tb], ALU.mult).then_inc(shares, 1)
                dve.wait_ge(shares, n + 3)
                nc.vector.reciprocal(total[:, tb], total[:, tb]).then_inc(shares, 1)

            def softmax(b, first):
                v = scores_v(b)
                nc.vector.tensor_tensor(mask[:], am[:], pm[:, bass.ds(b, 1), :].broadcast_to([P, TT, NK]),
                                        ALU.min).then_inc(masked, 1)
                dve.wait_ge(masked, b + 1)
                for tb in range(TT):
                    for j in range(KT):
                        dve.wait_ge(v_filled, v + (tb * KT + j + 1))
                        nc.vector.scalar_tensor_tensor(
                            pr[:, tb, j * HB:(j + 1) * HB, :],
                            ps[:, 4 + j, 0:HW].rearrange("p (h n) -> p h n", h=HB), SCALE,
                            mask[:, tb, :].unsqueeze(1).broadcast_to([P, HB, NK]),
                            ALU.mult, ALU.add).then_inc(v_taken, 1)
                    dve.wait_ge(v_taken, v + (tb + 1) * KT)
                    nc.vector.tensor_reduce(top[:, tb], pr[:, tb], AX.X, ALU.max).then_inc(topped, 1)
                    if tb >= 1:
                        dve.wait_ge(topped, b * TT + tb)
                        shares_of(b, tb - 1)
                    if tb < 2 and not first:
                        mix(b - 1, tb)
                dve.wait_ge(topped, b * TT + TT)
                shares_of(b, TT - 1)

            def norms(b, par, stats_mv, rs, ready, done):
                dve.wait_ge(ready, b + 1)
                for tb in range(TT):
                    nc.vector.tensor_scalar(xn[par][:, tb, :], xn[par][:, tb, :], stats_mv[:, tb, 0:1],
                                            rs[:, tb:tb + 1], ALU.subtract, ALU.mult).then_inc(done, 1)

            def ffn_out(b, a, v, par):
                dve.wait_ge(a_taken, a + FFN)
                for tb in range(TT):
                    dve.wait_ge(v_filled, v + (tb + 1))
                    nc.vector.tensor_tensor(r_s[:, tb, :], r_s[:, tb, :], ps[:, 4 + tb, :], ALU.mult
                                            ).then_inc(v_taken, 1)
                    dve.wait_ge(v_taken, v + (tb + 1))
                    nc.vector.tensor_tensor(xn[par][:, tb, :], xn[par][:, tb, :], r_s[:, tb, :],
                                            ALU.add).then_inc(z3, 1)
                    dve.wait_ge(z3, b * TT + tb + 1)
                    nc.vector.bn_stats(gst6[:, tb, :], xn[par][:, tb, :]).then_inc(z3_stats, 1)
                    dve.wait_ge(z3_stats, b * (2 * TT) + 2 * tb + 1)
                    nc.vector.tensor_copy(tick[:], eps[:])
                    nc.vector.bn_aggr(gmv[:, tb, :], gst6[:, tb, :]).then_inc(z3_stats, 1)

            def attention_out(b, par):
                v = out_v(b)
                for tb in range(TT):
                    dve.wait_ge(v_filled, v + (tb + 1))
                    if tb == 0:
                        dve.wait_ge(biased, b * TT + TT)
                    nc.vector.tensor_tensor(xn[par][:, tb, :], xn[par][:, tb, :], ps[:, 4 + tb, :],
                                            ALU.add).then_inc(v_taken, 1)
                    dve.wait_ge(v_taken, v + (tb + 1))
                    nc.vector.bn_stats(st6[:, tb, :], xn[par][:, tb, :]).then_inc(z2_stats, 1)
                    dve.wait_ge(z2_stats, b * (2 * TT) + 2 * tb + 1)
                    nc.vector.tensor_copy(tick[:], eps[:])
                    nc.vector.bn_aggr(mv[:, tb, :], st6[:, tb, :]).then_inc(z2_stats, 1)

            def row(b, par):
                first = isinstance(b, int) and b == 0
                if not first:
                    norms(b - 1, 1 - par, mv, rstd, rstd2, normed2)
                softmax(b, first)
                if not first:
                    ffn_out(b - 1, front_a(b) + FRONT, scores_v(b) + TT * KT, 1 - par)
                    norms(b - 1, 1 - par, gmv, grstd, rstd3, normed3)
                attention_out(b, par)

            rows(row, dve)
            last = (NB - 1) % 2
            norms(NB - 1, last, mv, rstd, rstd2, normed2)
            mix(NB - 1, 0)
            mix(NB - 1, 1)
            ffn_out(NB - 1, LAST_A, LAST_V, last)
            norms(NB - 1, last, gmv, grstd, rstd3, normed3)

        @block.gpsimd
        def _(pool):
            nc.gpsimd.memset(kbd[:], 0.0).then_inc(zeroed, 1)
            nc.gpsimd.memset(x2t[:, :, 0:1], 0.0).then_inc(zeroed, 1)
            pool.wait_ge(w_loaded, 16 * len(loads))
            pool.wait_ge(v_taken, NB)

            def prepare(b, par):
                pool.wait_ge(a_filled, front_a(b) + KT)
                for tb in range(TT):
                    nc.gpsimd.tensor_tensor(xn[par][:, tb, :], xn[par][:, tb, :], bo_s[:], ALU.add).then_inc(biased, 1)
                nc.gpsimd.tensor_copy(v_cur[0:NK, :], v_all[0:NK, b, :]).then_inc(v_here, 1)

            def softmax(b):
                def centre(tb):
                    pool.wait_ge(topped, b * TT + tb + 1)
                    nc.gpsimd.tensor_tensor(pr[:, tb], pr[:, tb], top[:, tb].unsqueeze(2).broadcast_to([P, NH, NK]),
                                            ALU.subtract).then_inc(centred, 1)

                def weigh(tb):
                    pool.wait_ge(shares, (b * TT + tb) * 4 + 4)
                    nc.gpsimd.tensor_tensor(pr[:, tb], pr[:, tb], total[:, tb].unsqueeze(2).broadcast_to([P, NH, NK]),
                                            ALU.mult).then_inc(probs, 1)

                for tb in range(TT):
                    centre(tb)
                    if tb >= 1:
                        weigh(tb - 1)
                weigh(TT - 1)

            def squares(b, a):
                for j in range(KT):
                    pool.wait_ge(a_taken, a + (KT + j + 1))
                    nc.gpsimd.tensor_tensor(kf[:, j, :], kf[:, j, :], kf[:, j, :], ALU.mult).then_inc(squared, 1)

            def row(b, par):
                first = isinstance(b, int) and b == 0
                prepare(b, par)
                softmax(b)
                if not first:
                    squares(b - 1, front_a(b) + FRONT)

            rows(row, pool)
            squares(NB - 1, LAST_A)


def decoder_layer(nc, t, out):
    x = t["x"]
    ns = t["a_log"].shape[2]
    c_dram = nc.dram_tensor("c_rows", (ns, x.shape[1]), FP32).ap()
    x1 = nc.dram_tensor("x1", x.shape, FP32).ap()
    mamba_pass(nc, x, t["x_t"], c_dram, t["w_u"], t["w_res"], t["w_conv"], t["b_conv"], t["w_x"], t["w_dt"], t["a_log"],
               t["d_skip"], t["w_out"], t["ident"], x1)
    cross_attention_ffn_pass(nc, x1, t["ctx_t"], t["attn_mask"], t["pad_mask"], t["wq"], t["wk"], t["wv"], t["wo"],
                             t["bq"], t["bk"], t["bv"], t["bo"], t["wr"], t["wkf"], t["wvf"], t["mu_r"], t["mu_k"],
                             t["ident"], out)




def kernel(**inputs):
    import numpy as np
    import concourse.bacc as bacc
    from concourse.bass_utils import run_bass_kernel_spmd

    a = {k: np.asarray(v) for k, v in inputs.items()}

    def blocks(w, p=P):
        return np.ascontiguousarray(w.reshape(w.shape[0] // p, p, -1).transpose(1, 0, 2))

    di, dtr = a["L0_attn_W_dt"].shape
    ns = a["L0_attn_A_log"].shape[1]
    wxp = a["L0_attn_W_xproj"].T
    w_x = np.zeros((di, P), np.float32)
    w_x[:, :dtr] = wxp[:, :dtr]
    w_x[:, dtr + 1:dtr + 1 + 2 * ns] = wxp[:, dtr:]
    w_dt = np.zeros((P, di), np.float32)
    w_dt[:dtr] = a["L0_attn_W_dt"].T
    w_dt[dtr] = a["L0_attn_b_dt"]
    arrays = {
        "x": a["x"],
        "x_t": np.ascontiguousarray(a["x"].reshape(a["x"].shape[0], a["x"].shape[1], -1, P).transpose(0, 3, 2, 1)),
        "w_u": blocks(a["L0_attn_W_in"][:di].T),
        "w_res": np.ascontiguousarray(blocks(a["L0_attn_W_in"][di:].T).reshape(P, -1, di // P, P).transpose(2, 0, 1, 3)),
        "w_conv": blocks(a["L0_attn_W_conv"].reshape(di, -1)),
        "b_conv": np.ascontiguousarray(a["L0_attn_b_conv"].reshape(-1, P).T),
        "w_x": blocks(w_x),
        "w_dt": np.ascontiguousarray(w_dt.reshape(P, -1, P).transpose(1, 0, 2)),
        "a_log": blocks(a["L0_attn_A_log"]),
        "d_skip": np.ascontiguousarray(a["L0_attn_D"].reshape(-1, P).T),
        "w_out": blocks(a["L0_attn_W_out"].T),
        "ident": np.eye(P, dtype=np.float32),
    }
    column = lambda v: np.ascontiguousarray(v.reshape(-1, P).T)
    arrays.update({
        "ctx_t": blocks(a["ctx_1024"].reshape(-1, a["ctx_1024"].shape[2]).T),
        "attn_mask": blocks(a["mask_SxS2_bk1"]),
        "pad_mask": a["mask_BxS2_bf0"],
        "bv": a["L0_xattn_bv"], "bo": a["L0_xattn_bo"],
        "bq": column(a["L0_xattn_bq"]), "bk": column(a["L0_xattn_bk"]),
        "mu_r": column(a["L0_ffn_mu_r"]), "mu_k": column(a["L0_ffn_mu_k"]),
        "wq": blocks(a["L0_xattn_Wq"].T), "wk": blocks(a["L0_xattn_Wk"].T), "wv": blocks(a["L0_xattn_Wv"].T),
        "wo": blocks(a["L0_xattn_Wo"].T), "wr": blocks(a["L0_ffn_W_r"].T), "wkf": blocks(a["L0_ffn_W_k"].T),
        "wvf": blocks(a["L0_ffn_W_v"].T),
    })
    nc = bacc.Bacc("TRN2", target_bir_lowering=False, num_devices=1)
    t = {n: nc.dram_tensor(n, v.shape, mybir.dt.from_np(v.dtype), kind="ExternalInput").ap()
         for n, v in arrays.items()}
    out = nc.dram_tensor("out", a["x"].shape, FP32, kind="ExternalOutput").ap()
    decoder_layer(nc, t, out)
    r = run_bass_kernel_spmd(nc, [arrays], core_ids=[0])
    return r.results[0]["out"]
```
